# Optimizing a Trainium2 kernel written in Bass

```python
import numpy as np
import jax
import jax.numpy as jnp

def _softmax(x, axis=-1):
    return jax.nn.softmax(x, axis=axis)

def _gelu(x):
    return jax.nn.gelu(x, approximate=True)

def _silu(x):
    return jax.nn.silu(x)

def _sigmoid(x):
    return jax.nn.sigmoid(x)

def _layernorm(x, axis=-1, eps=1e-05):
    m = jnp.mean(x, axis=axis, keepdims=True)
    v = jnp.var(x, axis=axis, keepdims=True)
    return (x - m) / jnp.sqrt(v + eps)

def _scatter_add(tgt, idx, src, axis=0):
    return tgt.at[idx].add(src)

def _segment_sum(src, seg, n):
    return jax.ops.segment_sum(src, seg, n)
kernel_name = 'mk_prb_d1_jaxref_r8_792f6c'

def setup_inputs(seed: int=0):
    np.random.seed(seed)
    _w = jnp.asarray

    def _L0_attn_setup():
        import jax, jax.numpy as jnp
        import numpy as np
        DIM = 128
        HEADS = 16
        DIM_HEAD = DIM // HEADS
        LATENT = DIM // 4
        SCALE = DIM_HEAD ** (-0.5)
        key = jax.random.key(seed)
        ks = jax.random.split(key, 8)
        B, S = (2, 256)
        init = lambda k, shape, fan_in: jax.random.normal(k, shape, jnp.float32) * fan_in ** (-0.5)
        return {'x': jax.random.normal(ks[0], (B, S, DIM), jnp.float32), 'Wq': init(ks[1], (DIM, DIM), DIM), 'bq': jnp.zeros((DIM,), jnp.float32), 'Wl': init(ks[2], (DIM, LATENT), DIM), 'bl': jnp.zeros((LATENT,), jnp.float32), 'Wk': init(ks[3], (LATENT, DIM), LATENT), 'bk': jnp.zeros((DIM,), jnp.float32), 'Wv': init(ks[4], (LATENT, DIM), LATENT), 'bv': jnp.zeros((DIM,), jnp.float32), 'Wo': init(ks[5], (DIM, DIM), DIM), 'bo': jnp.zeros((DIM,), jnp.float32)}
    _L0_attn_in = _L0_attn_setup()

    def _L0_ffn_setup():
        import jax, jax.numpy as jnp
        import numpy as np
        B, S, H = (1, 128, 128)
        E = 128
        NEXP = 16
        TOPK = 2
        ALPHA = 1.702
        LIMIT = 7.0

        def _moe_forward(x, Wg, bg, Wgu, bgu, Wd, bd):
            b, s, h = x.shape
            xt = x.reshape(-1, h)
            logits = xt @ Wg.T + bg
            top_vals, top_idx = jax.lax.top_k(logits, TOPK)
            rw = jax.nn.softmax(top_vals.astype(jnp.float32), axis=-1).astype(xt.dtype)
            onehot = jax.nn.one_hot(top_idx, NEXP, dtype=xt.dtype)
            cw = jnp.einsum('tk,tke->te', rw, onehot)
            gu = jnp.einsum('th,ehf->tef', xt, Wgu) + bgu[None]
            gate = gu[..., ::2]
            up = gu[..., 1::2]
            gate = jnp.minimum(gate, LIMIT)
            up = jnp.clip(up, -LIMIT, LIMIT)
            glu = gate * jax.nn.sigmoid(gate * ALPHA)
            gated = (up + 1.0) * glu
            out_e = jnp.einsum('tef,efh->teh', gated, Wd) + bd[None]
            out = jnp.einsum('teh,te->th', out_e, cw)
            return out.reshape(b, s, h)
        key = jax.random.key(seed)
        ks = jax.random.split(key, 8)
        hidden_states = jax.random.normal(ks[0], (B, S, H), dtype=jnp.float32)
        Wg = jax.random.normal(ks[1], (NEXP, H), dtype=jnp.float32) / np.sqrt(H)
        bg = jax.random.normal(ks[2], (NEXP,), dtype=jnp.float32) * 0.01
        Wgu = jax.random.normal(ks[3], (NEXP, H, 2 * E), dtype=jnp.float32) / np.sqrt(H)
        bgu = jax.random.normal(ks[4], (NEXP, 2 * E), dtype=jnp.float32) * 0.01
        Wd = jax.random.normal(ks[5], (NEXP, E, H), dtype=jnp.float32) / np.sqrt(E)
        bd = jax.random.normal(ks[6], (NEXP, H), dtype=jnp.float32) * 0.01
        return {'hidden_states': hidden_states, 'Wg': Wg, 'bg': bg, 'Wgu': Wgu, 'bgu': bgu, 'Wd': Wd, 'bd': bd}
    _L0_ffn_in = _L0_ffn_setup()
    _d = {'L0_attn_x': _L0_attn_in['x'], 'L0_attn_Wq': _L0_attn_in['Wq'], 'L0_attn_bq': _L0_attn_in['bq'], 'L0_attn_Wl': _L0_attn_in['Wl'], 'L0_attn_bl': _L0_attn_in['bl'], 'L0_attn_Wk': _L0_attn_in['Wk'], 'L0_attn_bk': _L0_attn_in['bk'], 'L0_attn_Wv': _L0_attn_in['Wv'], 'L0_attn_bv': _L0_attn_in['bv'], 'L0_attn_Wo': _L0_attn_in['Wo'], 'L0_attn_bo': _L0_attn_in['bo'], 'L0_ffn_Wg': _L0_ffn_in['Wg'], 'L0_ffn_bg': _L0_ffn_in['bg'], 'L0_ffn_Wgu': _L0_ffn_in['Wgu'], 'L0_ffn_bgu': _L0_ffn_in['bgu'], 'L0_ffn_Wd': _L0_ffn_in['Wd'], 'L0_ffn_bd': _L0_ffn_in['bd']}
    _x0 = _d['L0_attn_x']
    _d['L0_attn_x'] = jax.random.normal(jax.random.fold_in(jax.random.key(seed), 1), (2, 1024, 128), dtype=_x0.dtype)
    del _x0
    return _d

def reference(L0_attn_x, L0_attn_Wq, L0_attn_bq, L0_attn_Wl, L0_attn_bl, L0_attn_Wk, L0_attn_bk, L0_attn_Wv, L0_attn_bv, L0_attn_Wo, L0_attn_bo, L0_ffn_Wg, L0_ffn_bg, L0_ffn_Wgu, L0_ffn_bgu, L0_ffn_Wd, L0_ffn_bd):

    def _L0_attn_ref(x, Wq, bq, Wl, bl, Wk, bk, Wv, bv, Wo, bo):
        import jax, jax.numpy as jnp
        import numpy as np
        DIM = 128
        HEADS = 16
        DIM_HEAD = DIM // HEADS
        LATENT = DIM // 4
        SCALE = DIM_HEAD ** (-0.5)
        B, S, D = x.shape
        H, Dh = (HEADS, DIM_HEAD)
        q = (x @ Wq + bq).reshape(B, S, H, Dh)
        latent = x @ Wl + bl
        k = (latent @ Wk + bk).reshape(B, S, H, Dh)
        v = (latent @ Wv + bv).reshape(B, S, H, Dh)
        scores = jnp.einsum('bihd,bjhd->bhij', q, k) * SCALE
        attn = jax.nn.softmax(scores, axis=-1)
        out = jnp.einsum('bhij,bjhd->bihd', attn, v).reshape(B, S, D)
        out = out @ Wo + bo
        return out

    def _L0_ffn_ref(hidden_states, Wg, bg, Wgu, bgu, Wd, bd):
        import jax, jax.numpy as jnp
        import numpy as np
        B, S, H = (1, 128, 128)
        E = 128
        NEXP = 16
        TOPK = 2
        ALPHA = 1.702
        LIMIT = 7.0

        def _moe_forward(x, Wg, bg, Wgu, bgu, Wd, bd):
            b, s, h = x.shape
            xt = x.reshape(-1, h)
            logits = xt @ Wg.T + bg
            top_vals, top_idx = jax.lax.top_k(logits, TOPK)
            rw = jax.nn.softmax(top_vals.astype(jnp.float32), axis=-1).astype(xt.dtype)
            onehot = jax.nn.one_hot(top_idx, NEXP, dtype=xt.dtype)
            cw = jnp.einsum('tk,tke->te', rw, onehot)
            gu = jnp.einsum('th,ehf->tef', xt, Wgu) + bgu[None]
            gate = gu[..., ::2]
            up = gu[..., 1::2]
            gate = jnp.minimum(gate, LIMIT)
            up = jnp.clip(up, -LIMIT, LIMIT)
            glu = gate * jax.nn.sigmoid(gate * ALPHA)
            gated = (up + 1.0) * glu
            out_e = jnp.einsum('tef,efh->teh', gated, Wd) + bd[None]
            out = jnp.einsum('teh,te->th', out_e, cw)
            return out.reshape(b, s, h)
        return _moe_forward(hidden_states, Wg, bg, Wgu, bgu, Wd, bd)
    x = L0_attn_x
    xn = _layernorm(x, axis=-1)
    x = x + _L0_attn_ref(xn, L0_attn_Wq, L0_attn_bq, L0_attn_Wl, L0_attn_bl, L0_attn_Wk, L0_attn_bk, L0_attn_Wv, L0_attn_bv, L0_attn_Wo, L0_attn_bo) + _L0_ffn_ref(xn, L0_ffn_Wg, L0_ffn_bg, L0_ffn_Wgu, L0_ffn_bgu, L0_ffn_Wd, L0_ffn_bd)
    return x

_drawn_inputs = setup_inputs


def setup_inputs(seed=0):
    import zlib

    import numpy as np

    out = dict(_drawn_inputs(seed))
    spreads = {'L0_attn_bq': (0.0, 0.647),
     'L0_attn_bl': (0.0, 0.1),
     'L0_attn_bk': (0.0, 0.8),
     'L0_attn_bv': (0.0, 0.1),
     'L0_attn_bo': (0.0, 0.1)}
    factors = {'L0_ffn_bgu': 8.0, 'L0_ffn_bd': 8.0}
    for name, (base, spread) in spreads.items():
        noise = np.random.default_rng([zlib.crc32(name.encode()), seed]).standard_normal(out[name].shape)
        drawn = base * np.exp(spread * noise) if base else spread * noise
        out[name] = jnp.asarray(drawn.astype(out[name].dtype))
    for name, factor in factors.items():
        out[name] = (out[name] * factor).astype(out[name].dtype)
    return out
```

```python
from contextlib import ExitStack

import concourse.bass as bass
from concourse import mybir

P = 128
B, S, D = 2, 1024, 128
HEADS, DH, LATENT = 16, 8, 32
NEXP = 16
LIMIT, ALPHA, EPS = 7.0, 1.702, 1e-5
SCALE = float(DH) ** -0.5

TILES = B * S // P
CHUNKS = B * S // 512
PER_CHUNK = 4
HG = 4
NG = HEADS // HG
PG = B * NG
KB = S // P
PARTS = 3
PROD = PARTS * PARTS * DH
ROWS = PROD + PARTS
LEAD = 12
STEPS = 4 * KB
TURNS = PG // 2
RING = 3

ALU = mybir.AluOpType
ACT = mybir.ActivationFunctionType
AX_X = mybir.AxisListType.X
F32 = mybir.dt.float32
BF16 = mybir.dt.bfloat16
U32 = mybir.dt.uint32


def has_max(s, last):
    return not last or s + LEAD < STEPS


def has_turn(s, last):
    return s % KB == 5 and has_max(s - 2, last)


def has_sums(s):
    return s % KB == 2 and s >= KB


def has_proj(s):
    return s % KB == 4 and s >= KB


def jobs_before(s, last):
    return sum(4 * has_max(i, last) + has_turn(i, last) + has_sums(i) + has_proj(i) for i in range(s))


AHEAD_JOBS = 4 * LEAD + 1
TURN_OF_FIRST = 4 * 10
TURN_JOBS = jobs_before(STEPS, False) + 2


def moe_attention_kernel(nc, x, wq, bq, wl, bl, wk, bk, wv, wo, wg, bg, wexp, bgu, bdo, ident, sums_sel, iota, out):
    q_parts = nc.dram_tensor("q_parts", (PG, PARTS, DH * HG, S), BF16, kind="Internal").ap()
    k_parts = nc.dram_tensor("k_parts", (PG, PARTS, DH * HG, S), BF16, kind="Internal").ap()
    max_rows = nc.dram_tensor("max_rows", (2, PARTS * HG * 4, P), BF16, kind="Internal").ap()
    cw_rows = nc.dram_tensor("cw_rows", (NEXP, B * S), F32, kind="Internal").ap()

    with ExitStack() as ctx:
        def sb(name, shape, dt=F32):
            return ctx.enter_context(nc.sbuf_tensor(name, shape, dt))

        def sem(name):
            return ctx.enter_context(nc.semaphore(name))

        id_f = sb("id_f", [P, P])
        id_b = sb("id_b", [P, P], BF16)
        sel = sb("sel", [P, P])
        iota_e = sb("iota_e", [P, NEXP])
        wq_sb = sb("wq_sb", [P, D])
        wl_sb = sb("wl_sb", [P, LATENT])
        wk_sb = sb("wk_sb", [LATENT, D])
        wv_sb = sb("wv_sb", [LATENT + 1, D])
        wo_sb = sb("wo_sb", [P, PG, D])
        wg_sb = sb("wg_sb", [P, NEXP])
        bg_sb = sb("bg_sb", [1, NEXP])
        bq_sb = sb("bq_sb", [P, 1])
        bl_sb = sb("bl_sb", [LATENT, 1])
        bk_sb = sb("bk_sb", [P, 1])
        bdo_sb = sb("bdo_sb", [33, D])
        bgu_sb = sb("bgu_sb", [P, 2, NEXP])
        up_lo = sb("up_lo", [P, NEXP])
        up_hi = sb("up_hi", [P, NEXP])
        up_b1 = sb("up_b1", [P, NEXP])
        ones = sb("ones", [1, P])
        zeros = sb("zeros", [P, 16])
        y = sb("y", [P, TILES, D])
        xn = sb("xn", [P, TILES, D])
        xnT = sb("xnT", [P, B * S])
        stats = sb("stats", [P, TILES, 6])
        mv = sb("mv", [P, TILES, 2])
        rs = sb("rs", [P, 4, TILES])
        latT = sb("latT", [LATENT + 1, B * S])
        qf = sb("qf", [P, 2, 512])
        kf = sb("kf", [P, 2, 512])
        rq = sb("rq", [P, 512])
        rk = sb("rk", [P, 512])
        q3 = sb("q3", [P, 2, PARTS, 512], BF16)
        k3 = sb("k3", [P, 2, PARTS, 512], BF16)
        v_all = sb("v_all", [P, PG, KB, HG * DH])
        logits = sb("logits", [P, TILES, NEXP])
        top_v = sb("top_v", [P, TILES, 8])
        top_i = sb("top_i", [P, TILES, 8], U32)
        top_f = sb("top_f", [P, TILES, 2])
        tw = sb("tw", [P, 4, TILES])
        hot1 = sb("hot1", [P, TILES, NEXP])
        hot2 = sb("hot2", [P, TILES, NEXP])
        cw = sb("cw", [P, TILES, NEXP])
        cwT = sb("cwT", [33, B * S])
        cwT_half = sb("cwT_half", [NEXP, B * S])
        w_e = sb("w_e", [P, 2, 3, P])
        cw_e = sb("cw_e", [P, 2, B * S])
        gate = sb("gate", [P, 2, 512])
        up = sb("up", [P, 2, 512])
        th = sb("th", [P, 2, 512])
        glu = sb("glu", [P, 512])
        gated = sb("gated", [P, 2, 512])
        gw = sb("gw", [P, 2, 512])
        q_rows = [sb(f"q_rows{i}", [ROWS, HG, S], BF16) for i in range(2)]
        k_rows = [sb(f"k_rows{i}", [ROWS, HG, S], BF16) for i in range(2)]
        v_pad = sb("v_pad", [P, 2, KB, HG, 32])
        probs = sb("probs", [P, 4, 2, 512])
        half_max = sb("half_max", [P, 2, 16, 2])
        neg_max = sb("neg_max", [P, 2, 16])
        max_rest = sb("max_rest", [P, 16])
        max3_pad = sb("max3_pad", [P, 2, P], BF16)
        max3 = max3_pad[:, :, 0:PARTS * 16].rearrange("p u (a r) -> p u a r", a=PARTS)
        maxT = sb("maxT", [PARTS * 16, 2, P], BF16)
        pv_sb = sb("pv_sb", [P, 2, 512])
        sum_inv = sb("sum_inv", [P, 512])
        attnT = sb("attnT", [P, 2, 512])

        banks = ctx.enter_context(nc.psum_tensor("banks", [P, 8, 512], F32))

        s_x = [sem(f"s_x{c}") for c in range(CHUNKS)]
        s_id = sem("s_id")
        s_w = sem("s_w")
        s_dve = sem("s_dve")
        s_pool = sem("s_pool")
        s_var = sem("s_var")
        s_sqrt = sem("s_sqrt")
        s_xn = sem("s_xn")
        s_xt_ps = sem("s_xt_ps")
        s_xnT = sem("s_xnT")
        s_idb = sem("s_idb")
        s_rows1 = sem("s_rows1")
        s_lg = sem("s_lg")
        s_lg_sb = sem("s_lg_sb")
        s_lat_ps = sem("s_lat_ps")
        s_lat = sem("s_lat")
        s_q_ps = sem("s_q_ps")
        s_q = sem("s_q")
        s_k_ps = sem("s_k_ps")
        s_k = sem("s_k")
        s_v_ps = sem("s_v_ps")
        s_v = sem("s_v")
        s_q3 = sem("s_q3")
        s_k3 = sem("s_k3")
        s_q3_out = [sem(f"s_q3_out{i}") for i in range(2)]
        s_k3_out = [sem(f"s_k3_out{i}") for i in range(2)]
        s_gap = sem("s_gap")
        s_egap = sem("s_egap")
        s_cw = sem("s_cw")
        s_cwT_ps = sem("s_cwT_ps")
        s_cwT = sem("s_cwT")
        s_half = sem("s_half")
        s_cw_out = sem("s_cw_out")
        s_bgu = sem("s_bgu")
        s_we = [sem(f"s_we{i}") for i in range(2)]
        s_cwe = [sem(f"s_cwe{i}") for i in range(2)]
        s_gate_ps = sem("s_gate_ps")
        s_up_ps = sem("s_up_ps")
        s_gate = sem("s_gate")
        s_up = sem("s_up")
        s_th = sem("s_th")
        s_glu = sem("s_glu")
        s_gated = sem("s_gated")
        s_gw = sem("s_gw")
        s_down = sem("s_down")
        s_moe = sem("s_moe")
        s_krow1 = sem("s_krow1")
        s_qk = [sem(f"s_qk{i}") for i in range(2)]
        s_vz = sem("s_vz")
        s_vpad = sem("s_vpad")
        ring_full = sem("ring_full")
        ring_free = sem("ring_free")
        s_negmax = sem("s_negmax")
        s_max3 = sem("s_max3")
        s_maxout = sem("s_maxout")
        s_maxin = [sem(f"s_maxin{i}") for i in range(2)]
        s_scores = sem("s_scores")
        s_exp = sem("s_exp")
        s_pv = sem("s_pv")
        s_pv_sb = sem("s_pv_sb")
        s_attn = sem("s_attn")
        s_out = sem("s_out")

        QK_DMAS = 2 * PARTS * PARTS

        def turn_base(turn):
            return AHEAD_JOBS + TURN_JOBS * turn

        def expert_front(n):
            return n % 4, (n // 4) % 2

        block = ctx.enter_context(nc.Block())

        @block.sync
        def _(sp):
            xv = x.rearrange("b (t p) d -> p (b t) d", p=P)
            ov = out.rearrange("b (t p) d -> p (b t) d", p=P)
            for c in range(CHUNKS):
                sp.dma_start(y[:, 4 * c:4 * c + 4, :], xv[:, 4 * c:4 * c + 4, :]).then_inc(s_x[c], 16)

            def load_expert(e, slot):
                sp.dma_start(w_e[:, slot, :, :], wexp[bass.ds(e, 1), :, :, :].rearrange("o p a n -> p (o a) n")).then_inc(s_we[slot], 16)

            def load_cw(e, slot):
                sp.dma_start(cw_e[:, slot, :], cw_rows[bass.ds(e, 1), :].to_broadcast([P, B * S])).then_inc(s_cwe[slot], 16)

            def load_group(g, slot):
                for a in range(PARTS):
                    for c in range(PARTS):
                        r = DH * (PARTS * a + c)
                        sp.dma_start(k_rows[slot][r:r + DH, :, :].rearrange("d j t -> d (j t)"),
                                     k_parts[bass.ds(g, 1), a, :, :].rearrange("o (d j) t -> (o d) (j t)", j=HG)).then_inc(s_qk[slot], 16)
                        sp.dma_start(q_rows[slot][r:r + DH, :, :].rearrange("d j t -> d (j t)"),
                                     q_parts[bass.ds(g, 1), c, :, :].rearrange("o (d j) t -> (o d) (j t)", j=HG)).then_inc(s_qk[slot], 16)

            def load_max(parity, slot, half, done):
                sp.dma_start(max_rows[parity], maxT[:, parity, :]).then_inc(s_maxout, 16)
                sp.wait_ge(s_maxout, 16 * done)
                sp.dma_start(q_rows[slot][PROD:ROWS, :, 512 * half:512 * half + 512],
                             max_rows[parity].rearrange("(a j q) t -> a j (q t)", a=PARTS, j=HG)).then_inc(s_maxin[parity], 16)

            for e in range(2):
                load_expert(e, e)
            for c in range(CHUNKS):
                b, t0 = c // 2, 512 * (c % 2)
                for n, (parts, ready, dst, done) in enumerate(((q3, s_q3, q_parts, s_q3_out), (k3, s_k3, k_parts, s_k3_out))):
                    sp.wait_ge(ready, c + 1)
                    for g in range(NG):
                        sp.dma_start(dst[NG * b + g, :, :, t0:t0 + 512].rearrange("a r t -> r a t"),
                                     parts[32 * g:32 * g + 32, c % 2, :, :]).then_inc(done[c % 2], 16)
            sp.wait_ge(s_half, 1)
            sp.dma_start(cw_rows, cwT_half[:, :]).then_inc(s_cw_out, 16)
            sp.wait_ge(s_cw_out, 16)
            for e in range(2):
                load_cw(e, e)
            for i in range(2):
                sp.wait_ge(s_q3_out[i], 16 * 2 * NG)
                sp.wait_ge(s_k3_out[i], 16 * 2 * NG)
            sp.wait_ge(s_krow1, 2)
            with sp.Fori(0, NEXP // 2 - 1) as i:
                for k in range(2):
                    sp.wait_ge(s_down, 8 * i + 4 * k + 4 + 2)
                    load_expert(2 * i + 2 + k, k)
                    sp.wait_ge(s_gw, 8 * i + 4 * k + 4 + 2)
                    load_cw(2 * i + 2 + k, k)
            for slot in range(2):
                load_group(slot, slot)

            sp.wait_ge(ring_free, TURN_OF_FIRST + 1)
            load_max(0, 0, 0, 1)

            def turn(t, last):
                for s in range(STEPS):
                    if s == STEPS // 2 and not last:
                        sp.wait_ge(s_scores, 2 * STEPS * t + STEPS)
                        load_group(2 * t + 2, 0)
                    if has_turn(s, last):
                        unit = (s + LEAD - 2) // KB
                        sp.wait_ge(ring_free, turn_base(t) + jobs_before(s, last) + 4 * has_max(s, last) + 1)
                        load_max(unit % 2, (unit // 2) % 2, unit % 2, 4 * t + unit + 1)
                if not last:
                    sp.wait_ge(s_scores, 2 * STEPS * t + 2 * STEPS)
                    load_group(2 * t + 3, 1)

            with sp.Fori(0, TURNS - 1) as t:
                turn(t, False)
            sp.wait_ge(ring_free, turn_base(TURNS // 2))
            sp.dma_start(ov[:, 0:8, :], y[:, 0:8, :]).then_inc(s_out, 16)
            turn(TURNS - 1, True)
            sp.wait_ge(ring_free, turn_base(TURNS - 1) + jobs_before(29, True))
            sp.dma_start(ov[:, 8:12, :], y[:, 8:12, :]).then_inc(s_out, 16)
            sp.wait_ge(ring_free, turn_base(TURNS - 1) + jobs_before(STEPS, True) + 2)
            sp.dma_start(ov[:, 12:16, :], y[:, 12:16, :]).then_inc(s_out, 16)
            sp.wait_ge(s_out, 48)

        @block.gpsimd
        def _(pool):
            chain = [0]

            def link(ins):
                chain[0] += 1
                ins.then_inc(s_pool, 1)
                pool.wait_ge(s_pool, chain[0])

            for dst, src in ((bq_sb, bq), (bl_sb, bl), (bk_sb, bk), (wl_sb, wl), (wk_sb, wk), (wv_sb, wv), (wq_sb, wq),
                             (wg_sb, wg), (bg_sb, bg), (iota_e, iota), (bdo_sb, bdo), (bgu_sb, bgu), (sel, sums_sel), (wo_sb, wo)):
                pool.dma_start(dst[:], src).then_inc(s_w, 16)
            nc.gpsimd.memset(latT[LATENT:LATENT + 1, :], 1.0).then_inc(s_rows1, 1)
            pool.wait_ge(s_rows1, 1)
            nc.gpsimd.memset(ones[:], 1.0).then_inc(s_rows1, 1)
            pool.wait_ge(s_rows1, 2)
            link(nc.gpsimd.memset(cwT[:], 0.0))
            nc.gpsimd.memset(cwT[32:33, :], 1.0).then_inc(s_rows1, 1)
            pool.wait_ge(s_rows1, 3)
            for slot in range(2):
                nc.gpsimd.memset(k_rows[slot][64:ROWS, :, :], 1.0).then_inc(s_krow1, 1)
                pool.wait_ge(s_krow1, slot + 1)
            link(nc.gpsimd.memset(v_pad[:], 0.0))
            link(nc.gpsimd.memset(v_pad[:, :, :, :, DH:DH + 1], 1.0))
            link(nc.gpsimd.memset(max3_pad[:], 0.0))
            link(nc.gpsimd.memset(zeros[:], 0.0))

            for c in range(CHUNKS):
                i = c % 2
                pool.wait_ge(s_k, c + 1)
                if c >= 2:
                    pool.wait_ge(s_k3_out[i], 16 * NG)
                link(nc.gpsimd.tensor_copy(k3[:, i, 0, :], kf[:, i, :]))
                link(nc.gpsimd.tensor_tensor(rk[:], kf[:, i, :], k3[:, i, 0, :], ALU.subtract))
                link(nc.gpsimd.tensor_copy(k3[:, i, 1, :], rk[:]))
                nc.gpsimd.tensor_tensor(k3[:, i, 2, :], rk[:], k3[:, i, 1, :], ALU.subtract).then_inc(s_k3, 1)
                if c < CHUNKS - 1:
                    pool.wait_ge(s_k3, c + 1)

            def fill_v(g, slot):
                pool.wait_ge(s_v, CHUNKS)
                nc.gpsimd.tensor_copy(
                    v_pad[:, slot, :, :, 0:DH],
                    v_all[:, bass.ds(g, 1), :, :].rearrange("p o k (j d) -> p (o k) j d", d=DH)).then_inc(s_vpad, 1)

            fill_v(0, 0)
            fill_v(1, 1)

            nc.gpsimd.memset(max_rest[:], 0.0).then_inc(s_gw, 2)

            def weigh(i, n):
                c, slot = expert_front(n)
                if c == 0:
                    pool.wait_ge(s_cwe[slot], 16 * i + 16)
                pool.wait_ge(s_gated, 8 * i + n + 1 + 2)
                pool.wait_ge(s_down, 8 * i + n + 1)
                nc.gpsimd.tensor_tensor(gw[:, n % 2, :], gated[:, n % 2, :], cw_e[:, slot, 512 * c:512 * c + 512],
                                        ALU.mult).then_inc(s_gw, 1)

            with pool.Fori(0, NEXP // 2) as i:
                for n in range(8):
                    weigh(i, n)

            def split_max(parity, done):
                pool.wait_ge(s_negmax, done)
                base = 3 * (done - 1)
                nc.gpsimd.tensor_tensor(max3[:, parity, 0, :], neg_max[:, parity, :], zeros[:], ALU.add).then_inc(s_vz, 1)
                pool.wait_ge(s_vz, base + 1)
                nc.gpsimd.tensor_tensor(max_rest[:], neg_max[:, parity, :], max3[:, parity, 0, :], ALU.subtract).then_inc(s_vz, 1)
                pool.wait_ge(s_vz, base + 2)
                nc.gpsimd.tensor_tensor(max3[:, parity, 1, :], max_rest[:], zeros[:], ALU.add).then_inc(s_vz, 1)
                pool.wait_ge(s_vz, base + 3)
                nc.gpsimd.tensor_tensor(max3[:, parity, 2, :], max_rest[:], max3[:, parity, 1, :], ALU.subtract).then_inc(s_max3, 1)
                pool.wait_ge(s_max3, done)

            pool.wait_ge(s_gw, 8 * NEXP // 2 + 2)
            split_max(0, 1)

            def normalise(job, unit):
                pool.wait_ge(ring_free, job + 1)
                nc.gpsimd.tensor_tensor(attnT[:, unit % 2, :], pv_sb[:, unit % 2, :], sum_inv[:], ALU.mult).then_inc(s_attn, 1)

            def turn(t, last):
                for s in range(STEPS):
                    if has_sums(s):
                        normalise(turn_base(t) + jobs_before(s, last) + 4 * has_max(s, last), s // KB - 1)
                    if has_turn(s, last):
                        unit = (s + LEAD - 2) // KB
                        split_max(unit % 2, 4 * t + unit + 1)
                    if s == 22 and not last:
                        pool.wait_ge(s_pv, STEPS * t + STEPS // 2)
                        fill_v(2 * t + 2, 0)
                normalise(turn_base(t) + jobs_before(STEPS, last), 3)
                if not last:
                    pool.wait_ge(s_pv, STEPS * t + STEPS)
                    fill_v(2 * t + 3, 1)

            with pool.Fori(0, TURNS - 1) as t:
                turn(t, False)
            turn(TURNS - 1, True)

        @block.scalar
        def _(act):
            act.dma_start(id_f[:], ident).then_inc(s_id, 16)
            act.wait_ge(s_var, 1)
            nc.scalar.activation(rs[:, 1, :], rs[:, 0, :], ACT.Sqrt).then_inc(s_sqrt, 1)
            for c in range(CHUNKS):
                act.wait_ge(s_xt_ps, c + 1)
                nc.scalar.activation(xnT[:, 512 * c:512 * c + 512], banks[:, c, :], ACT.Copy).then_inc(s_xnT, 1)
            act.wait_ge(s_w, 16 * 14)
            for c in range(CHUNKS):
                if c == 1:
                    act.wait_ge(s_gap, 1)
                    nc.scalar.activation(tw[:, 1, :], tw[:, 0, :], ACT.Exp).then_inc(s_egap, 1)
                cols = slice(512 * c, 512 * c + 512)
                act.wait_ge(s_lat_ps, c + 1)
                nc.scalar.activation(latT[0:LATENT, cols], banks[0:LATENT, 4, :], ACT.Identity, bias=bl_sb[:, 0:1]).then_inc(s_lat, 1)
                act.wait_ge(s_q_ps, c + 1)
                if c >= 2:
                    act.wait_ge(s_q3, c - 1)
                nc.scalar.activation(qf[:, c % 2, :], banks[:, 5, :], ACT.Identity, bias=bq_sb[:, 0:1]).then_inc(s_q, 1)
                act.wait_ge(s_k_ps, c + 1)
                if c >= 2:
                    act.wait_ge(s_k3, c - 1)
                nc.scalar.activation(kf[:, c % 2, :], banks[:, 6, :], ACT.Identity, bias=bk_sb[:, 0:1]).then_inc(s_k, 1)
            act.wait_ge(s_rows1, 3)
            for c in range(CHUNKS):
                act.wait_ge(s_cwT_ps, c + 1)
                nc.scalar.activation(cwT[0:NEXP, 512 * c:512 * c + 512], banks[0:NEXP, c, :], ACT.Copy).then_inc(s_cwT, 1)
            act.wait_ge(s_cwT, CHUNKS)
            nc.scalar.activation(cwT_half[:, :], cwT[0:NEXP, :], ACT.Copy, scale=0.5).then_inc(s_half, 1)

            with act.Fori(0, NEXP // 2) as i:
                for n in range(8):
                    act.wait_ge(s_gate, 8 * i + n + 1)
                    act.wait_ge(s_glu, 8 * i + n + 1)
                    nc.scalar.activation(th[:, n % 2, :], gate[:, n % 2, :], ACT.Tanh, scale=ALPHA / 2).then_inc(s_th, 1)

            def keep_pv(unit, steps, units):
                act.wait_ge(s_pv, steps)
                nc.scalar.activation(pv_sb[:, unit % 2, :], banks[:, 4, :], ACT.Copy).then_inc(s_pv_sb, 1)

            def turn(t):
                for s in range(STEPS):
                    for pair in range(2):
                        n = 2 * s + pair
                        act.wait_ge(s_scores, 2 * STEPS * t + n + 1)
                        if s >= 2:
                            act.wait_ge(s_pv, STEPS * t + s - 1)
                        nc.scalar.activation(probs[:, n % 4, :, :], banks[:, 2 * pair:2 * pair + 2, :], ACT.Exp,
                                             scale=SCALE).then_inc(s_exp, 1)
                    if s % KB == 0 and s > 0:
                        keep_pv(s // KB - 1, STEPS * t + s, 4 * t + s // KB)
                keep_pv(3, STEPS * t + STEPS, 4 * t + 4)

            with act.Fori(0, TURNS) as t:
                turn(t)

        @block.vector
        def _(dve):
            chain = [0]

            def link(ins):
                chain[0] += 1
                ins.then_inc(s_dve, 1)
                dve.wait_ge(s_dve, chain[0])

            for c in range(CHUNKS):
                dve.wait_ge(s_x[c], 16)
                for t in range(4 * c, 4 * c + 4):
                    last = nc.vector.bn_stats(stats[:, t, :], y[:, t, :])
            link(last)
            for t in range(TILES):
                last = nc.vector.bn_aggr(mv[:, t, :], stats[:, t, :])
            link(last)
            nc.vector.tensor_scalar(rs[:, 0, :], mv[:, :, 1], EPS, None, ALU.add).then_inc(s_var, 1)
            dve.wait_ge(s_sqrt, 1)
            link(nc.vector.reciprocal(rs[:, 2, :], rs[:, 1, :]))
            link(nc.vector.tensor_tensor(rs[:, 3, :], rs[:, 2, :], rs[:, 2, :], ALU.mult))
            link(nc.vector.tensor_tensor(rs[:, 1, :], rs[:, 3, :], rs[:, 0, :], ALU.mult))
            link(nc.vector.tensor_scalar(rs[:, 3, :], rs[:, 1, :], -0.5, 1.5, ALU.mult, ALU.add))
            link(nc.vector.tensor_tensor(rs[:, 1, :], rs[:, 2, :], rs[:, 3, :], ALU.mult))
            for t in range(TILES):
                nc.vector.tensor_scalar(xn[:, t, :], y[:, t, :], mv[:, t, 0:1], rs[:, 1, t:t + 1],
                                        ALU.subtract, ALU.mult).then_inc(s_xn, 1)
            dve.wait_ge(s_id, 16)
            nc.vector.tensor_copy(id_b[:], id_f[:]).then_inc(s_idb, 1)
            dve.wait_ge(s_w, 16 * 14)
            nc.vector.tensor_scalar(up_lo[:], bgu_sb[:, 1, :], -1.0, -LIMIT, ALU.mult, ALU.add)
            nc.vector.tensor_scalar(up_hi[:], bgu_sb[:, 1, :], -1.0, LIMIT, ALU.mult, ALU.add)
            nc.vector.tensor_scalar(up_b1[:], bgu_sb[:, 1, :], 1.0, None, ALU.add).then_inc(s_bgu, 1)

            dve.wait_ge(s_lg, 1)
            link(nc.vector.tensor_copy(logits[:, :, :], banks[:, 0, 0:TILES * NEXP].rearrange("p (t e) -> p t e", e=NEXP)))
            for t in range(TILES):
                last = nc.vector.max(top_v[:, t, :], logits[:, t, :])
            link(last)
            nc.vector.tensor_tensor(tw[:, 0, :], top_v[:, :, 1], top_v[:, :, 0], ALU.subtract).then_inc(s_gap, 1)
            for t in range(TILES):
                last = nc.vector.max_index(top_i[:, t, :], top_v[:, t, :], logits[:, t, :])
            link(last)
            link(nc.vector.tensor_copy(top_f[:, :, :], top_i[:, :, 0:2]))
            dve.wait_ge(s_egap, 1)
            link(nc.vector.tensor_scalar(tw[:, 3, :], tw[:, 1, :], 1.0, None, ALU.add))
            link(nc.vector.reciprocal(tw[:, 2, :], tw[:, 3, :]))
            link(nc.vector.tensor_tensor(tw[:, 3, :], tw[:, 1, :], tw[:, 2, :], ALU.mult))
            experts = iota_e[:, None, :].to_broadcast([P, TILES, NEXP])
            for k, hot in ((0, hot1), (1, hot2)):
                link(nc.vector.tensor_tensor(hot[:, :, :], top_f[:, :, k:k + 1].to_broadcast([P, TILES, NEXP]), experts, ALU.is_equal))
                link(nc.vector.tensor_tensor(hot[:, :, :], hot[:, :, :],
                                             tw[:, 2 + k, :].unsqueeze(2).to_broadcast([P, TILES, NEXP]), ALU.mult))
            nc.vector.tensor_tensor(cw[:, :, :], hot1[:, :, :], hot2[:, :, :], ALU.add).then_inc(s_cw, 1)

            for c in range(CHUNKS):
                i = c % 2
                dve.wait_ge(s_v_ps, c + 1)
                nc.vector.tensor_copy(
                    v_all[:, NG * (c // 2):NG * (c // 2) + NG, 4 * i:4 * i + 4, :],
                    banks[:, 7, :].rearrange("p (k g n) -> p g k n", k=4, g=NG)).then_inc(s_v, 1)
                dve.wait_ge(s_q, c + 1)
                if c >= 2:
                    dve.wait_ge(s_q3_out[i], 16 * NG)
                link(nc.vector.tensor_copy(q3[:, i, 0, :], qf[:, i, :]))
                link(nc.vector.tensor_tensor(rq[:], qf[:, i, :], q3[:, i, 0, :], ALU.subtract))
                link(nc.vector.tensor_copy(q3[:, i, 1, :], rq[:]))
                nc.vector.tensor_tensor(q3[:, i, 2, :], rq[:], q3[:, i, 1, :], ALU.subtract).then_inc(s_q3, 1)
                if c < CHUNKS - 1:
                    dve.wait_ge(s_q3, c + 1)

            dve.wait_ge(s_bgu, 1)
            nc.vector.memset(glu[:, 0:1], 0.0).then_inc(s_glu, 2)
            nc.vector.memset(glu[:, 1:2], 0.0).then_inc(s_gated, 2)

            def gate_of(i, n):
                e = 2 * i + n // 4
                dve.wait_ge(s_gate_ps, 8 * i + n + 1)
                dve.wait_ge(s_glu, 8 * i + n - 1 + 2)
                nc.vector.tensor_scalar(gate[:, n % 2, :], banks[:, n % 2, :], bgu_sb[:, 0, bass.ds(e, 1)], LIMIT,
                                        ALU.add, ALU.min).then_inc(s_gate, 1)

            def up_of(i, n):
                e = 2 * i + n // 4
                dve.wait_ge(s_up_ps, 8 * i + n + 1)
                dve.wait_ge(s_gated, 8 * i + n - 1 + 2)
                nc.vector.tensor_scalar(up[:, n % 2, :], banks[:, 2 + n % 2, :], up_lo[:, bass.ds(e, 1)], up_hi[:, bass.ds(e, 1)],
                                        ALU.max, ALU.min).then_inc(s_up, 1)

            def glu_of(i, n):
                dve.wait_ge(s_th, 8 * i + n + 1)
                dve.wait_ge(s_gated, 8 * i + n + 2)
                nc.vector.scalar_tensor_tensor(out=glu[:], in0=th[:, n % 2, :], scalar=1.0, in1=gate[:, n % 2, :],
                                               op0=ALU.add, op1=ALU.mult).then_inc(s_glu, 1)

            def gated_of(i, n):
                e = 2 * i + n // 4
                dve.wait_ge(s_glu, 8 * i + n + 1 + 2)
                dve.wait_ge(s_gw, 8 * i + n + 1)
                nc.vector.scalar_tensor_tensor(out=gated[:, n % 2, :], in0=up[:, n % 2, :], scalar=up_b1[:, bass.ds(e, 1)],
                                               in1=glu[:], op0=ALU.add, op1=ALU.mult).then_inc(s_gated, 1)

            def pieces(i, last):
                for n in range(8):
                    if not (last and n == 7):
                        gate_of(i, n + 1)
                    glu_of(i, n)
                    if not (last and n == 7):
                        up_of(i, n + 1)
                    gated_of(i, n)

            dve.wait_ge(s_gated, 2)
            gate_of(0, 0)
            up_of(0, 0)
            with dve.Fori(0, NEXP // 2 - 1) as i:
                pieces(i, False)
            pieces(NEXP // 2 - 1, True)
            for c in range(CHUNKS):
                dve.wait_ge(s_down, 4 * (NEXP - 1) + c + 1 + 2)
                yc = y[:, 4 * c:4 * c + 4, :].rearrange("p t d -> p (t d)")
                nc.vector.tensor_tensor(yc, yc, banks[:, 4 + c, :], ALU.add).then_inc(s_moe, 1)
            dve.wait_ge(s_moe, CHUNKS)

            def max_jobs(base, job, ahead):
                unit = (ahead // KB) % 2
                for m in range(4):
                    row, half = divmod(4 * (ahead % KB) + m, 2)
                    dve.wait_ge(ring_full, base + job + m + 1)
                    nc.vector.tensor_reduce(half_max[:, unit, row, half:half + 1], banks[:, 5 + (job + m) % RING, :],
                                            AX_X, ALU.max).then_inc(ring_free, 1)
                if ahead % KB == KB - 1:
                    dve.wait_ge(ring_free, base + job + 4)
                    nc.vector.tensor_reduce(neg_max[:, unit, :], half_max[:, unit, :, :], AX_X, ALU.max,
                                            negate=True).then_inc(s_negmax, 1)

            def turned(base, job, unit):
                dve.wait_ge(ring_full, base + job + 1)
                nc.vector.tensor_copy(maxT[:, unit % 2, :],
                                      banks[0:PARTS * 16, 5 + job % RING, 0:P // 2].bitcast(BF16)).then_inc(ring_free, 1)

            def invert(base, job):
                dve.wait_ge(ring_full, base + job + 1)
                nc.vector.reciprocal(sum_inv[:], banks[:, 5 + job % RING, :]).then_inc(ring_free, 1)

            def add_out(base, job, t, unit):
                dve.wait_ge(ring_full, base + job + 1)
                yc = y[:, bass.ds((t // 2) * 8 + (unit % 2) * 4, 4), :]
                nc.vector.tensor_tensor(yc, yc, banks[:, 5 + job % RING, :].rearrange("p (t d) -> p t d", d=D),
                                        ALU.add).then_inc(ring_free, 1)

            for m in range(LEAD):
                max_jobs(0, 4 * m + (m >= 10), m)
                if m == 9:
                    turned(0, TURN_OF_FIRST, 0)

            def turn(t, last):
                base = turn_base(t)
                for s in range(STEPS):
                    job = jobs_before(s, last)
                    if has_max(s, last):
                        max_jobs(base, job, s + LEAD)
                        job += 4
                    if has_turn(s, last):
                        turned(base, job, (s + LEAD - 2) // KB)
                        job += 1
                    if has_sums(s):
                        invert(base, job)
                        job += 1
                    if has_proj(s):
                        add_out(base, job, t, s // KB - 1)
                        job += 1
                job = jobs_before(STEPS, last)
                invert(base, job)
                add_out(base, job + 1, t, 3)

            with dve.Fori(0, TURNS - 1) as t:
                turn(t, False)
            turn(TURNS - 1, True)

        @block.tensor
        def _(pe):
            pe.wait_ge(s_id, 16)
            for c in range(CHUNKS):
                pe.wait_ge(s_xn, 4 * c + 4)
                for t in range(4):
                    last = pe.transpose(banks[:, c, P * t:P * t + P], xn[:, 4 * c + t, :], id_f[:])
                last.then_inc(s_xt_ps, 1)
            pe.wait_ge(s_w, 16 * 14)
            pe.wait_ge(s_rows1, 3)
            pe.wait_ge(s_xnT, CHUNKS)
            for t in range(TILES):
                lg = banks[:, 0, NEXP * t:NEXP * t + NEXP]
                pe.matmul(lg, xnT[:, P * t:P * t + P], wg_sb[:], start=True, stop=False)
                last = pe.matmul(lg, ones[:], bg_sb[:], start=False, stop=True)
            last.then_inc(s_lg, 1)
            for c in range(CHUNKS):
                cols = slice(512 * c, 512 * c + 512)
                if c:
                    pe.wait_ge(s_lat, c)
                pe.matmul(banks[0:LATENT, 4, :], wl_sb[:], xnT[:, cols], start=True, stop=True).then_inc(s_lat_ps, 1)
                if c:
                    pe.wait_ge(s_q, c)
                pe.matmul(banks[:, 5, :], wq_sb[:], xnT[:, cols], start=True, stop=True).then_inc(s_q_ps, 1)
                pe.wait_ge(s_lat, c + 1)
                if c:
                    pe.wait_ge(s_k, c)
                pe.matmul(banks[:, 6, :], wk_sb[:], latT[0:LATENT, cols], start=True, stop=True).then_inc(s_k_ps, 1)
                if c:
                    pe.wait_ge(s_v, c)
                for t in range(4):
                    last = pe.matmul(banks[:, 7, P * t:P * t + P], latT[:, 512 * c + P * t:512 * c + P * t + P], wv_sb[:],
                                     start=True, stop=True)
                last.then_inc(s_v_ps, 1)
            pe.wait_ge(s_cw, 1)
            for c in range(CHUNKS):
                for t in range(4):
                    last = pe.transpose(banks[0:NEXP, c, P * t:P * t + P], cw[:, 4 * c + t, :], id_f[:])
                last.then_inc(s_cwT_ps, 1)
            pe.wait_ge(s_cwT, CHUNKS)
            pe.wait_ge(s_k, CHUNKS)
            pe.wait_ge(s_v, CHUNKS)
            for t in range(TILES):
                last = pe.matmul(banks[:, 4 + t // 4, P * (t % 4):P * (t % 4) + P], cwT[:, P * t:P * t + P], bdo_sb[:],
                                 start=(t % 4 == 0), stop=False, skip_group_check=True)
            last.then_inc(s_down, 2)

            def gate_up(i, n):
                c, slot = expert_front(n)
                cols = slice(512 * c, 512 * c + 512)
                if c == 0:
                    pe.wait_ge(s_we[slot], 16 * (i + n // 8) + 16)
                if not (isinstance(i, int) and i == 0 and n < 2):
                    pe.wait_ge(s_gate, 8 * i + n - 1)
                pe.matmul(banks[:, n % 2, :], w_e[:, slot, 0, :], xnT[:, cols], start=True, stop=True).then_inc(s_gate_ps, 1)
                if not (isinstance(i, int) and i == 0 and n < 2):
                    pe.wait_ge(s_up, 8 * i + n - 1)
                pe.matmul(banks[:, 2 + n % 2, :], w_e[:, slot, 1, :], xnT[:, cols], start=True, stop=True).then_inc(s_up_ps, 1)

            def down(i, n, last_expert):
                c, slot = expert_front(n)
                pe.wait_ge(s_gw, 8 * i + n + 1 + 2)
                for t in range(4):
                    mm = pe.matmul(banks[:, 4 + c, P * t:P * t + P], gw[:, n % 2, P * t:P * t + P], w_e[:, slot, 2, :],
                                   start=False, stop=last_expert, skip_group_check=True)
                mm.then_inc(s_down, 1)

            gate_up(0, 0)
            gate_up(0, 1)
            with pe.Fori(0, NEXP // 2 - 1) as i:
                for n in range(8):
                    gate_up(i, n + 2)
                    down(i, n, False)
            for n in range(8):
                if n < 6:
                    gate_up(NEXP // 2 - 1, n + 2)
                down(NEXP // 2 - 1, n, n >= 4)

            def ring_slot(base, job, first):
                if job >= RING:
                    pe.wait_ge(ring_free, base + job - RING + 1)
                elif not first:
                    pe.wait_ge(ring_free, base)
                return banks[:, 5 + job % RING, :]

            def max_jobs(base, job, ahead, first=False):
                unit = ahead // KB
                slot, half = (unit // 2) % 2, unit % 2
                for m in range(4):
                    row, keys = divmod(4 * (ahead % KB) + m, 2)
                    j, qb = divmod(row, 4)
                    bank = ring_slot(base, job + m, first)
                    q0 = 512 * half + P * qb
                    pe.matmul(bank, q_rows[slot][0:PROD, j, q0:q0 + P], k_rows[slot][0:PROD, j, 512 * keys:512 * keys + 512],
                              start=True, stop=True).then_inc(ring_full, 1)

            def turned(base, job, unit, done):
                pe.wait_ge(s_max3, done)
                bank = ring_slot(base, job, False)
                pe.transpose(bank[:, 0:P // 2].bitcast(BF16), max3_pad[:, unit % 2, :], id_b[:]).then_inc(ring_full, 1)

            def scores(t, s):
                unit, kb = divmod(s, KB)
                slot, half = unit // 2, unit % 2
                if kb == 0:
                    pe.wait_ge(s_maxin[half], 16 * (2 * t + unit // 2 + 1))
                for pair in range(2):
                    if s > 0:
                        pe.wait_ge(s_exp, 2 * STEPS * t + 2 * (s - 1) + pair + 1)
                    for j in (2 * pair, 2 * pair + 1):
                        mm = pe.matmul(banks[:, j, :], k_rows[slot][0:ROWS, j, P * kb:P * kb + P],
                                       q_rows[slot][0:ROWS, j, 512 * half:512 * half + 512], start=True, stop=True)
                    mm.then_inc(s_scores, 1)

            def values(t, s):
                unit, kb = divmod(s, KB)
                slot = unit // 2
                pe.wait_ge(s_exp, 2 * STEPS * t + 2 * s + 2)
                if kb == 0:
                    if unit > 0:
                        pe.wait_ge(s_pv_sb, 4 * t + unit)
                    pe.wait_ge(s_vpad, 2 * t + slot + 1)
                for j in range(HG):
                    mm = pe.matmul(banks[32 * j:32 * j + 32, 4, :], v_pad[:, slot, kb, j, :],
                                   probs[:, (2 * s + j // 2) % 4, j % 2, :], start=(kb == 0), stop=(kb == KB - 1))
                mm.then_inc(s_pv, 1)

            def sums(base, job, unit, done):
                pe.wait_ge(s_pv_sb, done)
                bank = ring_slot(base, job, False)
                pe.matmul(bank, sel[:], pv_sb[:, unit % 2, :], start=True, stop=True).then_inc(ring_full, 1)

            def project(base, job, t, unit):
                pe.wait_ge(s_attn, 4 * t + unit + 1)
                bank = ring_slot(base, job, False)
                for q in range(4):
                    mm = pe.matmul(bank[:, P * q:P * q + P], attnT[:, unit % 2, P * q:P * q + P],
                                   wo_sb[:, bass.ds(2 * t + unit // 2, 1), :].rearrange("p o n -> p (o n)"), start=True, stop=True)
                mm.then_inc(ring_full, 1)

            pe.wait_ge(s_moe, CHUNKS)
            pe.wait_ge(s_idb, 1)
            pe.wait_ge(s_qk[0], 16 * QK_DMAS)
            for m in range(LEAD):
                max_jobs(0, 4 * m + (m >= 10), m, m == 0)
                if m == 9:
                    turned(0, TURN_OF_FIRST, 0, 1)

            def turn(t, last):
                base = turn_base(t)
                for s in range(STEPS):
                    scores(t, s)
                    job = jobs_before(s, last)
                    if s == 4:
                        pe.wait_ge(s_qk[1], 16 * QK_DMAS * (t + 1))
                    if s == 20 and not last:
                        pe.wait_ge(s_qk[0], 16 * QK_DMAS * (t + 2))
                    if has_max(s, last):
                        max_jobs(base, job, s + LEAD)
                        job += 4
                    if s > 0:
                        values(t, s - 1)
                    if has_turn(s, last):
                        unit = (s + LEAD - 2) // KB
                        turned(base, job, unit, 4 * t + unit + 1)
                        job += 1
                    if has_sums(s):
                        sums(base, job, s // KB - 1, 4 * t + s // KB)
                        job += 1
                    if has_proj(s):
                        project(base, job, t, s // KB - 1)
                        job += 1
                values(t, STEPS - 1)
                job = jobs_before(STEPS, last)
                sums(base, job, 3, 4 * t + 4)
                project(base, job + 1, t, 3)

            with pe.Fori(0, TURNS - 1) as t:
                turn(t, False)
            turn(TURNS - 1, True)


def kernel(**inputs):
    import numpy as np

    import concourse.bacc as bacc
    from concourse.bass_utils import run_bass_kernel_spmd

    def f(name):
        return np.asarray(inputs[name])

    def by_group(a):
        return np.ascontiguousarray(a.reshape(a.shape[:-1] + (NG, HG, DH)).swapaxes(-1, -2).reshape(a.shape))

    wv = np.concatenate([f("L0_attn_Wv"), f("L0_attn_bv")[None, :]], 0)
    wo = np.zeros((PG, HG, 32, D), np.float32)
    wo[:, :, :DH, :] = np.concatenate([f("L0_attn_Wo").reshape(NG, HG, DH, D)] * B, 0)
    wo = np.ascontiguousarray(wo.reshape(PG, P, D).swapaxes(0, 1))
    wgu = f("L0_ffn_Wgu").reshape(NEXP, D, P, 2)
    wexp = np.ascontiguousarray(np.stack([wgu[..., 0], wgu[..., 1], f("L0_ffn_Wd")], 2))
    bgu = np.ascontiguousarray(f("L0_ffn_bgu").reshape(NEXP, P, 2).transpose(1, 2, 0))
    bdo = np.zeros((33, D), np.float32)
    bdo[:NEXP] = f("L0_ffn_bd")
    bdo[32] = f("L0_attn_bo")
    sums_sel = np.zeros((P, P), np.float32)
    for j in range(HG):
        sums_sel[32 * j + DH, 32 * j:32 * j + 32] = 1.0
    arrays = {
        "x": f("L0_attn_x"), "wq": by_group(f("L0_attn_Wq")), "bq": by_group(f("L0_attn_bq"))[:, None],
        "wl": f("L0_attn_Wl"), "bl": f("L0_attn_bl")[:, None], "wk": by_group(f("L0_attn_Wk")),
        "bk": by_group(f("L0_attn_bk"))[:, None], "wv": wv, "wo": wo,
        "wg": f("L0_ffn_Wg").T, "bg": f("L0_ffn_bg")[None, :], "wexp": wexp, "bgu": bgu, "bdo": bdo,
        "ident": np.eye(P, dtype=np.float32), "sums_sel": sums_sel,
        "iota": np.tile(np.arange(NEXP, dtype=np.float32), (P, 1)),
    }
    arrays = {n: np.ascontiguousarray(a) for n, a in arrays.items()}
    nc = bacc.Bacc("TRN2", target_bir_lowering=False, num_devices=1)
    args = [nc.dram_tensor(f"in_{n}", a.shape, F32, kind="ExternalInput").ap() for n, a in arrays.items()]
    out = nc.dram_tensor("out", (B, S, D), F32, kind="ExternalOutput").ap()
    moe_attention_kernel(nc, *args, out)
    r = run_bass_kernel_spmd(nc, [{f"in_{n}": a for n, a in arrays.items()}], core_ids=[0])
    return r.results[0]["out"]
```

```python
from contextlib import ExitStack

import concourse.bass as bass
from concourse import mybir

P = 128
B, S, D = 2, 1024, 128
HEADS, DH, LATENT = 16, 8, 32
NEXP = 16
LIMIT, ALPHA, EPS = 7.0, 1.702, 1e-5
SCALE = float(DH) ** -0.5

TILES = B * S // P
CHUNKS = B * S // 512
PER_CHUNK = 4
HG = 4
NG = HEADS // HG
PG = B * NG
KB = S // P
PARTS = 3
PROD = PARTS * PARTS * DH
ROWS = PROD + PARTS
LEAD = 12
STEPS = 4 * KB
TURNS = PG // 2
SLOTS = 4
FRONT = 3
RING = 3

ALU = mybir.AluOpType
ACT = mybir.ActivationFunctionType
AX_X = mybir.AxisListType.X
F32 = mybir.dt.float32
BF16 = mybir.dt.bfloat16
U32 = mybir.dt.uint32


def has_max(s, last):
    return not last or s + LEAD < STEPS


def has_max_turn(s, last):
    return s % KB == 5 and has_max(s - 2, last)


def has_value_turn(s):
    return s % KB == 2 and s >= KB


def jobs_before(s, start, last):
    return sum(4 * has_max(i, last) + has_max_turn(i, last) + has_value_turn(i) + 2 * (last and i in PROJECT)
               for i in range(start, s))


HEAD = 5
PROJECT = {20: (0, 0), 23: (0, 1), 29: (1, 0)}
TURN_OF_FIRST = 4 * 10
AHEAD_JOBS = 4 * LEAD + 1
BEFORE_JOBS = AHEAD_JOBS + jobs_before(HEAD, 0, False)
TURN_JOBS = jobs_before(STEPS + HEAD, HEAD, False)


def moe_attention_kernel(nc, x, wq, bq, wl, bl, wk, bk, wv, wo, wg, bg, wgu, wd, bdo, ident, iota, out):
    q_parts = nc.dram_tensor("q_parts", (PG, PARTS, DH * HG, S), BF16, kind="Internal").ap()
    k_parts = nc.dram_tensor("k_parts", (PG, PARTS, DH * HG, S), BF16, kind="Internal").ap()
    max_rows = nc.dram_tensor("max_rows", (2, PARTS * HG * 4, P), BF16, kind="Internal").ap()
    cw_rows = nc.dram_tensor("cw_rows", (NEXP, B * S), F32, kind="Internal").ap()

    with ExitStack() as ctx:
        def sb(name, shape, dt=F32):
            return ctx.enter_context(nc.sbuf_tensor(name, shape, dt))

        def sem(name):
            return ctx.enter_context(nc.semaphore(name))

        id_f = sb("id_f", [P, P])
        id_b = sb("id_b", [P, P], BF16)
        iota_e = sb("iota_e", [P, NEXP])
        wq_sb = sb("wq_sb", [P, D])
        wl_sb = sb("wl_sb", [P, LATENT])
        wk_sb = sb("wk_sb", [LATENT, D])
        wv_sb = sb("wv_sb", [LATENT + 1, D])
        wo_sb = sb("wo_sb", [P, D])
        wg_sb = sb("wg_sb", [P, NEXP])
        bg_sb = sb("bg_sb", [1, NEXP])
        bq_sb = sb("bq_sb", [P, 1])
        bl_sb = sb("bl_sb", [LATENT, 1])
        bk_sb = sb("bk_sb", [P, 1])
        bdo_sb = sb("bdo_sb", [33, D])
        ones = sb("ones", [1, P])
        zeros = sb("zeros", [P, 16])
        y = sb("y", [P, TILES, D])
        xn = sb("xn", [P, TILES, D])
        xnT = sb("xnT", [P, B * S])
        stats = sb("stats", [P, TILES, 6])
        mv = sb("mv", [P, TILES, 2])
        rs = sb("rs", [P, 4, TILES])
        latT = sb("latT", [LATENT + 1, B * S])
        qf = sb("qf", [P, 2, 512])
        kf = sb("kf", [P, 2, 512])
        rq = sb("rq", [P, 512])
        rk = sb("rk", [P, 512])
        q3 = sb("q3", [P, 2, PARTS, 512], BF16)
        k3 = sb("k3", [P, 2, PARTS, 512], BF16)
        v_all = sb("v_all", [P, PG, KB, HG * DH])
        logits = sb("logits", [P, TILES, NEXP])
        top_v = sb("top_v", [P, TILES, 8])
        top_i = sb("top_i", [P, TILES, 8], U32)
        top_f = sb("top_f", [P, TILES, 2])
        tw = sb("tw", [P, 4, TILES])
        hot1 = sb("hot1", [P, TILES, NEXP])
        hot2 = sb("hot2", [P, TILES, NEXP])
        cw = sb("cw", [P, TILES, NEXP])
        cwT = sb("cwT", [33, B * S])
        cwT_half = sb("cwT_half", [NEXP, B * S])
        wgu_e = sb("wgu_e", [P, 2, 2 * P + 2])
        wd_e = sb("wd_e", [P, 2, P])
        cw_e = sb("cw_e", [P, 2, B * S])
        gate = sb("gate", [P, SLOTS, 512])
        th = sb("th", [P, SLOTS, 512])
        up = sb("up", [P, SLOTS, 512])
        q_rows = [sb(f"q_rows{i}", [ROWS, HG, S], BF16) for i in range(2)]
        k_rows = [sb(f"k_rows{i}", [ROWS, HG, S], BF16) for i in range(2)]
        v_pad = sb("v_pad", [P, 2, KB, HG, 32])
        probs = sb("probs", [P, 4, 2, 512])
        half_max = sb("half_max", [P, 2, 16, 2])
        neg_max = sb("neg_max", [P, 2, 16])
        max_rest = sb("max_rest", [P, 16])
        max3_pad = sb("max3_pad", [P, 2, P], BF16)
        max3 = max3_pad[:, :, 0:PARTS * 16].rearrange("p u (a r) -> p u a r", a=PARTS)
        maxT = sb("maxT", [PARTS * 16, 2, P], BF16)
        pv_sb = sb("pv_sb", [P, 2, 512])
        sum_inv = sb("sum_inv", [P, 4, HG])
        attn = sb("attn", [P, TILES, NG, HG * DH])
        attnT = sb("attnT", [P, 512])

        banks = ctx.enter_context(nc.psum_tensor("banks", [P, 8, 512], F32))

        s_x = [sem(f"s_x{c}") for c in range(CHUNKS)]
        s_id = sem("s_id")
        s_w = sem("s_w")
        s_dve = sem("s_dve")
        s_pool = sem("s_pool")
        s_var = sem("s_var")
        s_sqrt = sem("s_sqrt")
        s_xn = sem("s_xn")
        s_xt_ps = sem("s_xt_ps")
        s_xnT = sem("s_xnT")
        s_idb = sem("s_idb")
        s_rows1 = sem("s_rows1")
        s_lg = sem("s_lg")
        s_lg_sb = sem("s_lg_sb")
        s_lat_ps = sem("s_lat_ps")
        s_lat = sem("s_lat")
        s_q_ps = sem("s_q_ps")
        s_q = sem("s_q")
        s_k_ps = sem("s_k_ps")
        s_k = sem("s_k")
        s_v_ps = sem("s_v_ps")
        s_v = sem("s_v")
        s_q3 = sem("s_q3")
        s_k3 = sem("s_k3")
        s_q3_out = [sem(f"s_q3_out{i}") for i in range(2)]
        s_k3_out = [sem(f"s_k3_out{i}") for i in range(2)]
        s_gap = sem("s_gap")
        s_egap = sem("s_egap")
        s_cw = sem("s_cw")
        s_cwT_ps = sem("s_cwT_ps")
        s_cwT = sem("s_cwT")
        s_half = sem("s_half")
        s_cw_out = sem("s_cw_out")
        s_wgu = [sem(f"s_wgu{i}") for i in range(2)]
        s_wd = [sem(f"s_wd{i}") for i in range(2)]
        s_cwe = [sem(f"s_cwe{i}") for i in range(2)]
        s_gate_ps = sem("s_gate_ps")
        s_up_ps = sem("s_up_ps")
        s_gate_in = sem("s_gate_in")
        s_up_in = sem("s_up_in")
        s_gate = sem("s_gate")
        s_up = sem("s_up")
        s_th = sem("s_th")
        s_glu = sem("s_glu")
        s_gated = sem("s_gated")
        s_down = sem("s_down")
        s_gw = sem("s_gw")
        s_moe = sem("s_moe")
        s_krow1 = sem("s_krow1")
        s_qk = [sem(f"s_qk{i}") for i in range(2)]
        s_vz = sem("s_vz")
        s_vpad = sem("s_vpad")
        ring_full = sem("ring_full")
        ring_free = sem("ring_free")
        s_negmax = sem("s_negmax")
        s_max3 = sem("s_max3")
        s_maxout = sem("s_maxout")
        s_maxin = [sem(f"s_maxin{i}") for i in range(2)]
        s_scores = sem("s_scores")
        s_exp = sem("s_exp")
        s_pv = sem("s_pv")
        s_pv_sb = sem("s_pv_sb")
        s_inv = sem("s_inv")
        s_out = sem("s_out")

        QK_DMAS = 2 * PARTS * PARTS

        def turn_base(turn):
            return BEFORE_JOBS + TURN_JOBS * turn

        def expert_front(n):
            return n % 4, (n // 4) % 2

        block = ctx.enter_context(nc.Block())

        @block.sync
        def _(sp):
            xv = x.rearrange("b (t p) d -> p (b t) d", p=P)
            ov = out.rearrange("b (t p) d -> p (b t) d", p=P)
            for c in range(CHUNKS):
                sp.dma_start(y[:, 4 * c:4 * c + 4, :], xv[:, 4 * c:4 * c + 4, :]).then_inc(s_x[c], 16)

            def load_gate_up(e, slot):
                sp.dma_start(wgu_e[:, slot, :], wgu[bass.ds(e, 1), :, :].rearrange("o p n -> (o p) n")).then_inc(s_wgu[slot], 16)

            def load_down(e, slot):
                sp.dma_start(wd_e[:, slot, :], wd[bass.ds(e, 1), :, :].rearrange("o p n -> (o p) n")).then_inc(s_wd[slot], 16)

            def load_cw(e, slot):
                sp.dma_start(cw_e[:, slot, :], cw_rows[bass.ds(e, 1), :].to_broadcast([P, B * S])).then_inc(s_cwe[slot], 16)

            def load_group(g, slot):
                for a in range(PARTS):
                    for c in range(PARTS):
                        r = DH * (PARTS * a + c)
                        sp.dma_start(k_rows[slot][r:r + DH, :, :].rearrange("d j t -> d (j t)"),
                                     k_parts[bass.ds(g, 1), a, :, :].rearrange("o (d j) t -> (o d) (j t)", j=HG)).then_inc(s_qk[slot], 16)
                        sp.dma_start(q_rows[slot][r:r + DH, :, :].rearrange("d j t -> d (j t)"),
                                     q_parts[bass.ds(g, 1), c, :, :].rearrange("o (d j) t -> (o d) (j t)", j=HG)).then_inc(s_qk[slot], 16)

            def load_max(parity, slot, half, done):
                sp.dma_start(max_rows[parity], maxT[:, parity, :]).then_inc(s_maxout, 16)
                sp.wait_ge(s_maxout, 16 * done)
                sp.dma_start(q_rows[slot][PROD:ROWS, :, 512 * half:512 * half + 512],
                             max_rows[parity].rearrange("(a j q) t -> a j (q t)", a=PARTS, j=HG)).then_inc(s_maxin[parity], 16)

            for e in range(2):
                load_gate_up(e, e)
                load_down(e, e)
            for c in range(CHUNKS):
                b, t0 = c // 2, 512 * (c % 2)
                for n, (parts, ready, dst, done) in enumerate(((q3, s_q3, q_parts, s_q3_out), (k3, s_k3, k_parts, s_k3_out))):
                    sp.wait_ge(ready, c + 1)
                    for g in range(NG):
                        sp.dma_start(dst[NG * b + g, :, :, t0:t0 + 512].rearrange("a r t -> r a t"),
                                     parts[32 * g:32 * g + 32, c % 2, :, :]).then_inc(done[c % 2], 16)
            sp.wait_ge(s_half, 1)
            sp.dma_start(cw_rows, cwT_half[:, :]).then_inc(s_cw_out, 16)
            sp.wait_ge(s_cw_out, 16)
            for e in range(2):
                load_cw(e, e)
            for i in range(2):
                sp.wait_ge(s_q3_out[i], 16 * 2 * NG)
                sp.wait_ge(s_k3_out[i], 16 * 2 * NG)
            sp.wait_ge(s_krow1, 2)
            with sp.Fori(0, NEXP // 2 - 1) as i:
                for k in range(2):
                    sp.wait_ge(s_up_in, 8 * i + 4 * k + 4)
                    load_gate_up(2 * i + 2 + k, k)
                    sp.wait_ge(s_gw, 8 * i + 4 * k + 4)
                    load_cw(2 * i + 2 + k, k)
                    sp.wait_ge(s_down, 8 * i + 4 * k + 4 + SLOTS)
                    load_down(2 * i + 2 + k, k)
            for slot in range(2):
                load_group(slot, slot)

            sp.wait_ge(ring_free, TURN_OF_FIRST + 1)
            load_max(0, 0, 0, 1)

            def turn(t, last):
                for s in range(HEAD, STEPS if last else STEPS + HEAD):
                    if s == STEPS // 2 and not last:
                        sp.wait_ge(s_scores, 2 * STEPS * t + STEPS)
                        load_group(2 * t + 2, 0)
                    if s == STEPS and not last:
                        sp.wait_ge(s_scores, 2 * STEPS * t + 2 * STEPS)
                        load_group(2 * t + 3, 1)
                    if has_max_turn(s, last):
                        unit = (s + LEAD - 2) // KB
                        sp.wait_ge(ring_free, turn_base(t) + jobs_before(s, HEAD, last) + 4 * has_max(s, last) + 1)
                        load_max(unit % 2, (unit // 2) % 2, unit % 2, 4 * t + unit + 1)
                    if last and s in PROJECT:
                        store(jobs_before(s + 1, HEAD, True), *PROJECT[s])

            def store(jobs, b, half):
                sp.wait_ge(ring_free, turn_base(TURNS - 1) + jobs)
                t0 = 8 * b + 4 * half
                sp.dma_start(ov[:, t0:t0 + 4, :], y[:, t0:t0 + 4, :]).then_inc(s_out, 16)

            with sp.Fori(0, TURNS - 1) as t:
                turn(t, False)
            turn(TURNS - 1, True)
            store(jobs_before(STEPS, HEAD, True) + 3, 1, 1)
            sp.wait_ge(s_out, 16 * 2 * B)

        @block.gpsimd
        def _(pool):
            chain = [0]

            def link(ins):
                chain[0] += 1
                ins.then_inc(s_pool, 1)
                pool.wait_ge(s_pool, chain[0])

            nc.gpsimd.memset(latT[LATENT:LATENT + 1, :], 1.0).then_inc(s_rows1, 1)
            pool.wait_ge(s_rows1, 1)
            nc.gpsimd.memset(ones[:], 1.0).then_inc(s_rows1, 1)
            pool.wait_ge(s_rows1, 2)
            link(nc.gpsimd.memset(cwT[:], 0.0))
            nc.gpsimd.memset(cwT[32:33, :], 1.0).then_inc(s_rows1, 1)
            pool.wait_ge(s_rows1, 3)
            for slot in range(2):
                nc.gpsimd.memset(k_rows[slot][64:ROWS, :, :], 1.0).then_inc(s_krow1, 1)
                pool.wait_ge(s_krow1, slot + 1)
            link(nc.gpsimd.memset(v_pad[:], 0.0))
            link(nc.gpsimd.memset(v_pad[:, :, :, :, DH:DH + 1], 1.0))
            link(nc.gpsimd.memset(max3_pad[:], 0.0))
            link(nc.gpsimd.memset(zeros[:], 0.0))

            for c in range(CHUNKS):
                i = c % 2
                pool.wait_ge(s_k, c + 1)
                if c >= 2:
                    pool.wait_ge(s_k3_out[i], 16 * NG)
                link(nc.gpsimd.tensor_copy(k3[:, i, 0, :], kf[:, i, :]))
                link(nc.gpsimd.tensor_tensor(rk[:], kf[:, i, :], k3[:, i, 0, :], ALU.subtract))
                link(nc.gpsimd.tensor_copy(k3[:, i, 1, :], rk[:]))
                nc.gpsimd.tensor_tensor(k3[:, i, 2, :], rk[:], k3[:, i, 1, :], ALU.subtract).then_inc(s_k3, 1)
                if c < CHUNKS - 1:
                    pool.wait_ge(s_k3, c + 1)

            def fill_v(g, slot):
                pool.wait_ge(s_v, CHUNKS)
                nc.gpsimd.tensor_copy(
                    v_pad[:, slot, :, :, 0:DH],
                    v_all[:, bass.ds(g, 1), :, :].rearrange("p o k (j d) -> p (o k) j d", d=DH)).then_inc(s_vpad, 1)

            fill_v(0, 0)
            fill_v(1, 1)

            def weigh(i, n):
                c, slot = expert_front(n)
                if c == 0:
                    pool.wait_ge(s_cwe[slot], 16 * i + 16)
                pool.wait_ge(s_gated, 8 * i + n + 1 + SLOTS)
                nc.gpsimd.tensor_tensor(up[:, n % SLOTS, :], up[:, n % SLOTS, :], cw_e[:, slot, 512 * c:512 * c + 512],
                                        ALU.mult).then_inc(s_gw, 1)

            with pool.Fori(0, NEXP // 2) as i:
                for n in range(8):
                    weigh(i, n)

            def split_max(parity, done):
                pool.wait_ge(s_negmax, done)
                base = 3 * (done - 1)
                nc.gpsimd.tensor_tensor(max3[:, parity, 0, :], neg_max[:, parity, :], zeros[:], ALU.add).then_inc(s_vz, 1)
                pool.wait_ge(s_vz, base + 1)
                nc.gpsimd.tensor_tensor(max_rest[:], neg_max[:, parity, :], max3[:, parity, 0, :], ALU.subtract).then_inc(s_vz, 1)
                pool.wait_ge(s_vz, base + 2)
                nc.gpsimd.tensor_tensor(max3[:, parity, 1, :], max_rest[:], zeros[:], ALU.add).then_inc(s_vz, 1)
                pool.wait_ge(s_vz, base + 3)
                nc.gpsimd.tensor_tensor(max3[:, parity, 2, :], max_rest[:], max3[:, parity, 1, :], ALU.subtract).then_inc(s_max3, 1)
                pool.wait_ge(s_max3, done)

            pool.wait_ge(s_gw, 8 * NEXP // 2)
            split_max(0, 1)

            def turn(t, last):
                for s in range(HEAD, STEPS if last else STEPS + HEAD):
                    if has_max_turn(s, last):
                        unit = (s + LEAD - 2) // KB
                        split_max(unit % 2, 4 * t + unit + 1)
                    if s == 22 and not last:
                        pool.wait_ge(s_pv, STEPS * t + STEPS // 2)
                        fill_v(2 * t + 2, 0)
                    if s == STEPS + 2:
                        pool.wait_ge(s_pv, STEPS * t + STEPS)
                        fill_v(2 * t + 3, 1)

            with pool.Fori(0, TURNS - 1) as t:
                turn(t, False)
            turn(TURNS - 1, True)

        @block.scalar
        def _(act):
            act.dma_start(id_f[:], ident).then_inc(s_id, 16)
            for dst, src in ((wg_sb, wg), (bg_sb, bg), (wl_sb, wl), (bl_sb, bl), (wq_sb, wq), (bq_sb, bq), (wk_sb, wk), (bk_sb, bk),
                             (wv_sb, wv), (iota_e, iota), (bdo_sb, bdo), (wo_sb, wo)):
                act.dma_start(dst[:], src).then_inc(s_w, 16)
            act.wait_ge(s_var, 1)
            nc.scalar.activation(rs[:, 1, :], rs[:, 0, :], ACT.Sqrt).then_inc(s_sqrt, 1)
            for c in range(CHUNKS):
                act.wait_ge(s_xt_ps, c + 1)
                nc.scalar.activation(xnT[:, 512 * c:512 * c + 512], banks[:, c, :], ACT.Copy).then_inc(s_xnT, 1)
            act.wait_ge(s_w, 16 * 12)
            for c in range(CHUNKS):
                if c == 1:
                    act.wait_ge(s_gap, 1)
                    nc.scalar.activation(tw[:, 1, :], tw[:, 0, :], ACT.Exp).then_inc(s_egap, 1)
                cols = slice(512 * c, 512 * c + 512)
                act.wait_ge(s_lat_ps, c + 1)
                nc.scalar.activation(latT[0:LATENT, cols], banks[0:LATENT, 4, :], ACT.Identity, bias=bl_sb[:, 0:1]).then_inc(s_lat, 1)
                act.wait_ge(s_q_ps, c + 1)
                if c >= 2:
                    act.wait_ge(s_q3, c - 1)
                nc.scalar.activation(qf[:, c % 2, :], banks[:, 5, :], ACT.Identity, bias=bq_sb[:, 0:1]).then_inc(s_q, 1)
                act.wait_ge(s_k_ps, c + 1)
                if c >= 2:
                    act.wait_ge(s_k3, c - 1)
                nc.scalar.activation(kf[:, c % 2, :], banks[:, 6, :], ACT.Identity, bias=bk_sb[:, 0:1]).then_inc(s_k, 1)
            act.wait_ge(s_rows1, 3)
            for c in range(CHUNKS):
                act.wait_ge(s_cwT_ps, c + 1)
                nc.scalar.activation(cwT[0:NEXP, 512 * c:512 * c + 512], banks[0:NEXP, c, :], ACT.Copy).then_inc(s_cwT, 1)
            act.wait_ge(s_cwT, CHUNKS)
            nc.scalar.activation(cwT_half[:, :], cwT[0:NEXP, :], ACT.Copy, scale=0.5).then_inc(s_half, 1)

            def gate_up_in(i, n):
                slot = expert_front(n)[1]
                act.wait_ge(s_gate_ps, 8 * i + n + 1)
                act.wait_ge(s_glu, 8 * i + n + 1)
                nc.scalar.activation(gate[:, n % SLOTS, :], banks[:, n % 2, :], ACT.Identity,
                                     bias=wgu_e[:, slot, 2 * P:2 * P + 1]).then_inc(s_gate_in, 1)
                act.wait_ge(s_up_ps, 8 * i + n + 1)
                act.wait_ge(s_down, 8 * i + n + 1)
                nc.scalar.activation(up[:, n % SLOTS, :], banks[:, 2 + n % 2, :], ACT.Identity,
                                     bias=wgu_e[:, slot, 2 * P + 1:2 * P + 2]).then_inc(s_up_in, 1)

            def tanh_of(i, n):
                act.wait_ge(s_gate, 8 * i + n + 1)
                act.wait_ge(s_gated, 8 * i + n + 1)
                nc.scalar.activation(th[:, n % SLOTS, :], gate[:, n % SLOTS, :], ACT.Tanh, scale=ALPHA / 2).then_inc(s_th, 1)

            def pieces(i, last):
                for n in range(8):
                    if not (last and n == 7):
                        gate_up_in(i, n + 1)
                    tanh_of(i, n)

            gate_up_in(0, 0)
            with act.Fori(0, NEXP // 2 - 1) as i:
                pieces(i, False)
            pieces(NEXP // 2 - 1, True)

            def keep_pv(t, unit):
                act.wait_ge(s_pv, STEPS * t + KB * (unit + 1))
                nc.scalar.activation(pv_sb[:, unit % 2, :], banks[:, 4, :], ACT.Copy).then_inc(s_pv_sb, 1)

            def exponentials(t, s):
                for pair in range(2):
                    n = 2 * s + pair
                    act.wait_ge(s_scores, 2 * STEPS * t + n + 1)
                    if s >= 2:
                        act.wait_ge(s_pv, STEPS * t + s - 1)
                    nc.scalar.activation(probs[:, n % 4, :, :], banks[:, 2 * pair:2 * pair + 2, :], ACT.Exp,
                                         scale=SCALE).then_inc(s_exp, 1)
                if s % KB == 0 and s > 0:
                    keep_pv(t, s // KB - 1)

            for s in range(HEAD):
                exponentials(0, s)
            with act.Fori(0, TURNS - 1) as t:
                for s in range(HEAD, STEPS + HEAD):
                    exponentials(t, s)
            for s in range(HEAD, STEPS):
                exponentials(TURNS - 1, s)
            keep_pv(TURNS - 1, 3)

        @block.vector
        def _(dve):
            chain = [0]

            def link(ins):
                chain[0] += 1
                ins.then_inc(s_dve, 1)
                dve.wait_ge(s_dve, chain[0])

            for c in range(CHUNKS):
                dve.wait_ge(s_x[c], 16)
                for t in range(4 * c, 4 * c + 4):
                    last = nc.vector.bn_stats(stats[:, t, :], y[:, t, :])
            link(last)
            for t in range(TILES):
                last = nc.vector.bn_aggr(mv[:, t, :], stats[:, t, :])
            link(last)
            nc.vector.tensor_scalar(rs[:, 0, :], mv[:, :, 1], EPS, None, ALU.add).then_inc(s_var, 1)
            dve.wait_ge(s_sqrt, 1)
            link(nc.vector.reciprocal(rs[:, 2, :], rs[:, 1, :]))
            link(nc.vector.tensor_tensor(rs[:, 3, :], rs[:, 2, :], rs[:, 2, :], ALU.mult))
            link(nc.vector.tensor_tensor(rs[:, 1, :], rs[:, 3, :], rs[:, 0, :], ALU.mult))
            link(nc.vector.tensor_scalar(rs[:, 3, :], rs[:, 1, :], -0.5, 1.5, ALU.mult, ALU.add))
            link(nc.vector.tensor_tensor(rs[:, 1, :], rs[:, 2, :], rs[:, 3, :], ALU.mult))
            for t in range(TILES):
                nc.vector.tensor_scalar(xn[:, t, :], y[:, t, :], mv[:, t, 0:1], rs[:, 1, t:t + 1],
                                        ALU.subtract, ALU.mult).then_inc(s_xn, 1)
            dve.wait_ge(s_id, 16)
            nc.vector.tensor_copy(id_b[:], id_f[:]).then_inc(s_idb, 1)
            dve.wait_ge(s_lg, 1)
            link(nc.vector.tensor_copy(logits[:, :, :], banks[:, 0, 0:TILES * NEXP].rearrange("p (t e) -> p t e", e=NEXP)))
            for t in range(TILES):
                last = nc.vector.max(top_v[:, t, :], logits[:, t, :])
            link(last)
            nc.vector.tensor_tensor(tw[:, 0, :], top_v[:, :, 1], top_v[:, :, 0], ALU.subtract).then_inc(s_gap, 1)
            for t in range(TILES):
                last = nc.vector.max_index(top_i[:, t, :], top_v[:, t, :], logits[:, t, :])
            link(last)
            link(nc.vector.tensor_copy(top_f[:, :, :], top_i[:, :, 0:2]))
            dve.wait_ge(s_egap, 1)
            link(nc.vector.tensor_scalar(tw[:, 3, :], tw[:, 1, :], 1.0, None, ALU.add))
            link(nc.vector.reciprocal(tw[:, 2, :], tw[:, 3, :]))
            link(nc.vector.tensor_tensor(tw[:, 3, :], tw[:, 1, :], tw[:, 2, :], ALU.mult))
            experts = iota_e[:, None, :].to_broadcast([P, TILES, NEXP])
            for k, hot in ((0, hot1), (1, hot2)):
                link(nc.vector.tensor_tensor(hot[:, :, :], top_f[:, :, k:k + 1].to_broadcast([P, TILES, NEXP]), experts, ALU.is_equal))
                link(nc.vector.tensor_tensor(hot[:, :, :], hot[:, :, :],
                                             tw[:, 2 + k, :].unsqueeze(2).to_broadcast([P, TILES, NEXP]), ALU.mult))
            nc.vector.tensor_tensor(cw[:, :, :], hot1[:, :, :], hot2[:, :, :], ALU.add).then_inc(s_cw, 1)

            for c in range(CHUNKS):
                i = c % 2
                dve.wait_ge(s_v_ps, c + 1)
                nc.vector.tensor_copy(
                    v_all[:, NG * (c // 2):NG * (c // 2) + NG, 4 * i:4 * i + 4, :],
                    banks[:, 7, :].rearrange("p (k g n) -> p g k n", k=4, g=NG)).then_inc(s_v, 1)
                dve.wait_ge(s_q, c + 1)
                if c >= 2:
                    dve.wait_ge(s_q3_out[i], 16 * NG)
                link(nc.vector.tensor_copy(q3[:, i, 0, :], qf[:, i, :]))
                link(nc.vector.tensor_tensor(rq[:], qf[:, i, :], q3[:, i, 0, :], ALU.subtract))
                link(nc.vector.tensor_copy(q3[:, i, 1, :], rq[:]))
                nc.vector.tensor_tensor(q3[:, i, 2, :], rq[:], q3[:, i, 1, :], ALU.subtract).then_inc(s_q3, 1)
                if c < CHUNKS - 1:
                    dve.wait_ge(s_q3, c + 1)

            nc.vector.memset(th[:, 0, 0:1], 0.0).then_inc(s_glu, SLOTS)
            nc.vector.memset(th[:, 1, 0:1], 0.0).then_inc(s_gated, SLOTS)

            def gate_of(i, n):
                g = gate[:, n % SLOTS, :]
                dve.wait_ge(s_gate_in, 8 * i + n + 1)
                nc.vector.tensor_scalar(g, g, LIMIT, None, ALU.min).then_inc(s_gate, 1)

            def up_of(i, n):
                u = up[:, n % SLOTS, :]
                dve.wait_ge(s_up_in, 8 * i + n + 1)
                nc.vector.tensor_scalar(u, u, -LIMIT, LIMIT, ALU.max, ALU.min).then_inc(s_up, 1)

            def glu_of(i, n):
                dve.wait_ge(s_th, 8 * i + n + 1)
                nc.vector.scalar_tensor_tensor(out=th[:, n % SLOTS, :], in0=th[:, n % SLOTS, :], scalar=1.0,
                                               in1=gate[:, n % SLOTS, :], op0=ALU.add, op1=ALU.mult).then_inc(s_glu, 1)

            def gated_of(i, n):
                dve.wait_ge(s_up, 8 * i + n + 1)
                dve.wait_ge(s_glu, 8 * i + n + 1 + SLOTS)
                nc.vector.scalar_tensor_tensor(out=up[:, n % SLOTS, :], in0=up[:, n % SLOTS, :], scalar=1.0,
                                               in1=th[:, n % SLOTS, :], op0=ALU.add, op1=ALU.mult).then_inc(s_gated, 1)

            def pieces(i, last):
                for n in range(8):
                    if not (last and n == 7):
                        gate_of(i, n + 1)
                    glu_of(i, n)
                    if not (last and n == 7):
                        up_of(i, n + 1)
                    gated_of(i, n)

            dve.wait_ge(s_gated, SLOTS)
            gate_of(0, 0)
            up_of(0, 0)
            with dve.Fori(0, NEXP // 2 - 1) as i:
                pieces(i, False)
            pieces(NEXP // 2 - 1, True)
            for c in range(CHUNKS):
                dve.wait_ge(s_down, 4 * (NEXP - 1) + c + 1 + SLOTS)
                yc = y[:, 4 * c:4 * c + 4, :].rearrange("p t d -> p (t d)")
                nc.vector.tensor_tensor(yc, yc, banks[:, 4 + c, :], ALU.add).then_inc(s_moe, 1)
            dve.wait_ge(s_moe, CHUNKS)

            def max_jobs(base, job, ahead):
                unit = (ahead // KB) % 2
                for m in range(4):
                    row, half = divmod(4 * (ahead % KB) + m, 2)
                    dve.wait_ge(ring_full, base + job + m + 1)
                    nc.vector.tensor_reduce(half_max[:, unit, row, half:half + 1], banks[:, 5 + (job + m) % RING, :],
                                            AX_X, ALU.max).then_inc(ring_free, 1)
                if ahead % KB == KB - 1:
                    dve.wait_ge(ring_free, base + job + 4)
                    nc.vector.tensor_reduce(neg_max[:, unit, :], half_max[:, unit, :, :], AX_X, ALU.max,
                                            negate=True).then_inc(s_negmax, 1)

            def maxima_turned(base, job, unit):
                dve.wait_ge(ring_full, base + job + 1)
                nc.vector.tensor_copy(maxT[:, unit % 2, :],
                                      banks[0:PARTS * 16, 5 + job % RING, 0:P // 2].bitcast(BF16)).then_inc(ring_free, 1)

            def normalise(base, job, t, unit):
                rows = banks[:, 5 + job % RING, :].rearrange("p (q j m) -> p q j m", q=4, j=HG)
                dve.wait_ge(ring_full, base + job + 1)
                nc.vector.reciprocal(sum_inv[:, :, :], rows[:, :, :, DH]).then_inc(s_inv, 1)
                dve.wait_ge(s_inv, 4 * t + unit + 1)
                nc.vector.tensor_tensor(
                    attn[:, bass.ds((t // 2) * 8 + (unit % 2) * 4, 4), bass.ds((t % 2) * 2 + unit // 2, 1), :].rearrange(
                        "p q o (j d) -> p q (o j) d", d=DH),
                    rows[:, :, :, 0:DH], sum_inv[:, :, :].unsqueeze(3).to_broadcast([P, 4, HG, DH]),
                    ALU.mult).then_inc(ring_free, 1)

            def rows_turned(base, job):
                dve.wait_ge(ring_full, base + job + 1)
                nc.vector.tensor_copy(attnT[:, :], banks[:, 5 + job % RING, :]).then_inc(ring_free, 1)

            def add_out(base, job, b, half):
                dve.wait_ge(ring_full, base + job + 1)
                t0 = 8 * b + 4 * half
                yc = y[:, t0:t0 + 4, :].rearrange("p t d -> p (t d)")
                nc.vector.tensor_tensor(yc, yc, banks[:, 5 + job % RING, :], ALU.add).then_inc(ring_free, 1)

            for m in range(LEAD):
                max_jobs(0, 4 * m + (m >= 10), m)
                if m == 9:
                    maxima_turned(0, TURN_OF_FIRST, 0)

            def step(base, job, t, s, last):
                if has_max(s, last):
                    max_jobs(base, job, s + LEAD)
                    job += 4
                if has_max_turn(s, last):
                    maxima_turned(base, job, (s + LEAD - 2) // KB)
                    job += 1
                if has_value_turn(s):
                    normalise(base, job, t, s // KB - 1)
                    job += 1
                if last and s in PROJECT:
                    rows_turned(base, job)
                    add_out(base, job + 1, *PROJECT[s])

            for s in range(HEAD):
                step(0, AHEAD_JOBS + jobs_before(s, 0, False), 0, s, False)
            with dve.Fori(0, TURNS - 1) as t:
                for s in range(HEAD, STEPS + HEAD):
                    step(turn_base(t), jobs_before(s, HEAD, False), t, s, False)
            base = turn_base(TURNS - 1)
            for s in range(HEAD, STEPS):
                step(base, jobs_before(s, HEAD, True), TURNS - 1, s, True)
            job = jobs_before(STEPS, HEAD, True)
            normalise(base, job, TURNS - 1, 3)
            rows_turned(base, job + 1)
            add_out(base, job + 2, 1, 1)

        @block.tensor
        def _(pe):
            pe.wait_ge(s_id, 16)
            for c in range(CHUNKS):
                pe.wait_ge(s_xn, 4 * c + 4)
                for t in range(4):
                    last = pe.transpose(banks[:, c, P * t:P * t + P], xn[:, 4 * c + t, :], id_f[:])
                last.then_inc(s_xt_ps, 1)
            pe.wait_ge(s_w, 16 * 12)
            pe.wait_ge(s_rows1, 3)
            pe.wait_ge(s_xnT, CHUNKS)
            for t in range(TILES):
                lg = banks[:, 0, NEXP * t:NEXP * t + NEXP]
                pe.matmul(lg, xnT[:, P * t:P * t + P], wg_sb[:], start=True, stop=False)
                last = pe.matmul(lg, ones[:], bg_sb[:], start=False, stop=True)
            last.then_inc(s_lg, 1)
            for c in range(CHUNKS):
                cols = slice(512 * c, 512 * c + 512)
                if c:
                    pe.wait_ge(s_lat, c)
                pe.matmul(banks[0:LATENT, 4, :], wl_sb[:], xnT[:, cols], start=True, stop=True).then_inc(s_lat_ps, 1)
                if c:
                    pe.wait_ge(s_q, c)
                pe.matmul(banks[:, 5, :], wq_sb[:], xnT[:, cols], start=True, stop=True).then_inc(s_q_ps, 1)
                pe.wait_ge(s_lat, c + 1)
                if c:
                    pe.wait_ge(s_k, c)
                pe.matmul(banks[:, 6, :], wk_sb[:], latT[0:LATENT, cols], start=True, stop=True).then_inc(s_k_ps, 1)
                if c:
                    pe.wait_ge(s_v, c)
                for t in range(4):
                    last = pe.matmul(banks[:, 7, P * t:P * t + P], latT[:, 512 * c + P * t:512 * c + P * t + P], wv_sb[:],
                                     start=True, stop=True)
                last.then_inc(s_v_ps, 1)
            pe.wait_ge(s_cw, 1)
            for c in range(CHUNKS):
                for t in range(4):
                    last = pe.transpose(banks[0:NEXP, c, P * t:P * t + P], cw[:, 4 * c + t, :], id_f[:])
                last.then_inc(s_cwT_ps, 1)
            pe.wait_ge(s_cwT, CHUNKS)
            pe.wait_ge(s_k, CHUNKS)
            pe.wait_ge(s_v, CHUNKS)
            for t in range(TILES):
                last = pe.matmul(banks[:, 4 + t // 4, P * (t % 4):P * (t % 4) + P], cwT[:, P * t:P * t + P], bdo_sb[:],
                                 start=(t % 4 == 0), stop=False, skip_group_check=True)
            last.then_inc(s_down, SLOTS)

            def gate_up(i, n):
                c, slot = expert_front(n)
                cols = slice(512 * c, 512 * c + 512)
                if c == 0:
                    pe.wait_ge(s_wgu[slot], 16 * (i + n // 8) + 16)
                if not (isinstance(i, int) and i == 0 and n < 2):
                    pe.wait_ge(s_gate_in, 8 * i + n - 1)
                pe.matmul(banks[:, n % 2, :], wgu_e[:, slot, 0:P], xnT[:, cols], start=True, stop=True).then_inc(s_gate_ps, 1)
                if not (isinstance(i, int) and i == 0 and n < 2):
                    pe.wait_ge(s_up_in, 8 * i + n - 1)
                pe.matmul(banks[:, 2 + n % 2, :], wgu_e[:, slot, P:2 * P], xnT[:, cols], start=True, stop=True).then_inc(s_up_ps, 1)

            def down(i, n, last_expert):
                c, slot = expert_front(n)
                if c == 0:
                    pe.wait_ge(s_wd[slot], 16 * i + 16)
                pe.wait_ge(s_gw, 8 * i + n + 1)
                for t in range(4):
                    mm = pe.matmul(banks[:, 4 + c, P * t:P * t + P], up[:, n % SLOTS, P * t:P * t + P], wd_e[:, slot, :],
                                   start=False, stop=last_expert, skip_group_check=True)
                mm.then_inc(s_down, 1)

            for n in range(FRONT):
                gate_up(0, n)
            with pe.Fori(0, NEXP // 2 - 1) as i:
                for n in range(8):
                    gate_up(i, n + FRONT)
                    down(i, n, False)
            for n in range(8):
                if n < 8 - FRONT:
                    gate_up(NEXP // 2 - 1, n + FRONT)
                down(NEXP // 2 - 1, n, n >= 4)

            def ring_slot(base, job, first):
                if job >= RING:
                    pe.wait_ge(ring_free, base + job - RING + 1)
                elif not first:
                    pe.wait_ge(ring_free, base)
                return banks[:, 5 + job % RING, :]

            def max_job(base, job, ahead, m, first=False):
                unit = ahead // KB
                slot, half = (unit // 2) % 2, unit % 2
                row, keys = divmod(4 * (ahead % KB) + m, 2)
                j, qb = divmod(row, 4)
                bank = ring_slot(base, job + m, first)
                q0 = 512 * half + P * qb
                pe.matmul(bank, q_rows[slot][0:PROD, j, q0:q0 + P], k_rows[slot][0:PROD, j, 512 * keys:512 * keys + 512],
                          start=True, stop=True).then_inc(ring_full, 1)

            def turn_maxima(base, job, unit, done):
                pe.wait_ge(s_max3, done)
                bank = ring_slot(base, job, False)
                pe.transpose(bank[:, 0:P // 2].bitcast(BF16), max3_pad[:, unit % 2, :], id_b[:]).then_inc(ring_full, 1)

            def scores(t, s, pair):
                unit, kb = divmod(s, KB)
                slot, half = (unit // 2) % 2, unit % 2
                if kb == 0 and pair == 0:
                    pe.wait_ge(s_maxin[half], 16 * (2 * t + unit // 2 + 1))
                if s > 0:
                    pe.wait_ge(s_exp, 2 * STEPS * t + 2 * (s - 1) + pair + 1)
                for j in (2 * pair, 2 * pair + 1):
                    mm = pe.matmul(banks[:, j, :], k_rows[slot][0:ROWS, j, P * kb:P * kb + P],
                                   q_rows[slot][0:ROWS, j, 512 * half:512 * half + 512], start=True, stop=True)
                mm.then_inc(s_scores, 1)

            def values(t, s):
                unit, kb = divmod(s, KB)
                slot = (unit // 2) % 2
                pe.wait_ge(s_exp, 2 * STEPS * t + 2 * s + 2)
                if kb == 0:
                    if unit > 0:
                        pe.wait_ge(s_pv_sb, 4 * t + unit)
                    pe.wait_ge(s_vpad, 2 * t + unit // 2 + 1)
                for j in range(HG):
                    mm = pe.matmul(banks[32 * j:32 * j + 32, 4, :], v_pad[:, slot, kb, j, :],
                                   probs[:, (2 * s + j // 2) % 4, j % 2, :], start=(kb == 0), stop=(kb == KB - 1))
                mm.then_inc(s_pv, 1)

            def turn_values(base, job, t, unit):
                pe.wait_ge(s_pv_sb, 4 * t + unit + 1)
                bank = ring_slot(base, job, False)
                for q in range(4):
                    mm = pe.transpose(bank[:, P * q:P * q + P], pv_sb[:, unit % 2, P * q:P * q + P], id_f[:])
                mm.then_inc(ring_full, 1)

            def turn_rows(base, job, b, half):
                pe.wait_ge(ring_free, base + job)
                bank = ring_slot(base, job, False)
                for q in range(4):
                    mm = pe.transpose(bank[:, P * q:P * q + P], attn[:, 8 * b + 4 * half + q, :, :].rearrange("p g n -> p (g n)"), id_f[:])
                mm.then_inc(ring_full, 1)

            def project(base, job):
                pe.wait_ge(ring_free, base + job)
                bank = ring_slot(base, job, False)
                for q in range(4):
                    mm = pe.matmul(bank[:, P * q:P * q + P], attnT[:, P * q:P * q + P], wo_sb[:], start=True, stop=True)
                mm.then_inc(ring_full, 1)

            pe.wait_ge(s_moe, CHUNKS)
            pe.wait_ge(s_idb, 1)
            pe.wait_ge(s_qk[0], 16 * QK_DMAS)
            for m in range(LEAD):
                for k in range(4):
                    max_job(0, 4 * m + (m >= 10), m, k, m == 0)
                if m == 9:
                    turn_maxima(0, TURN_OF_FIRST, 0, 1)

            def step(base, job, t, s, last):
                if s == 4:
                    pe.wait_ge(s_qk[1], 16 * QK_DMAS)
                if s == 20 and not last:
                    pe.wait_ge(s_qk[0], 16 * QK_DMAS * (t + 2))
                if s == 36:
                    pe.wait_ge(s_qk[1], 16 * QK_DMAS * (t + 2))
                maxima = has_max(s, last)
                scores(t, s, 0)
                if maxima:
                    max_job(base, job, s + LEAD, 0)
                scores(t, s, 1)
                if maxima:
                    max_job(base, job, s + LEAD, 1)
                if s > 0:
                    values(t, s - 1)
                if maxima:
                    max_job(base, job, s + LEAD, 2)
                    max_job(base, job, s + LEAD, 3)
                    job += 4
                if has_max_turn(s, last):
                    unit = (s + LEAD - 2) // KB
                    turn_maxima(base, job, unit, 4 * t + unit + 1)
                    job += 1
                if has_value_turn(s):
                    turn_values(base, job, t, s // KB - 1)
                    job += 1
                if last and s in PROJECT:
                    turn_rows(base, job, *PROJECT[s])
                    project(base, job + 1)

            for s in range(HEAD):
                step(0, AHEAD_JOBS + jobs_before(s, 0, False), 0, s, False)
            with pe.Fori(0, TURNS - 1) as t:
                for s in range(HEAD, STEPS + HEAD):
                    step(turn_base(t), jobs_before(s, HEAD, False), t, s, False)
            base = turn_base(TURNS - 1)
            for s in range(HEAD, STEPS):
                step(base, jobs_before(s, HEAD, True), TURNS - 1, s, True)
            values(TURNS - 1, STEPS - 1)
            job = jobs_before(STEPS, HEAD, True)
            turn_values(base, job, TURNS - 1, 3)
            turn_rows(base, job + 1, 1, 1)
            project(base, job + 2)


def kernel(**inputs):
    import numpy as np

    import concourse.bacc as bacc
    from concourse.bass_utils import run_bass_kernel_spmd

    def f(name):
        return np.asarray(inputs[name])

    def by_group(a):
        return np.ascontiguousarray(a.reshape(a.shape[:-1] + (NG, HG, DH)).swapaxes(-1, -2).reshape(a.shape))

    wv = np.concatenate([f("L0_attn_Wv"), f("L0_attn_bv")[None, :]], 0)
    wgu = f("L0_ffn_Wgu").reshape(NEXP, D, P, 2).swapaxes(2, 3).reshape(NEXP, D, 2 * P)
    wgu = np.concatenate([wgu, f("L0_ffn_bgu").reshape(NEXP, P, 2)], 2)
    bdo = np.zeros((33, D), np.float32)
    bdo[:NEXP] = f("L0_ffn_bd")
    bdo[32] = f("L0_attn_bo")
    arrays = {
        "x": f("L0_attn_x"), "wq": by_group(f("L0_attn_Wq")), "bq": by_group(f("L0_attn_bq"))[:, None],
        "wl": f("L0_attn_Wl"), "bl": f("L0_attn_bl")[:, None], "wk": by_group(f("L0_attn_Wk")),
        "bk": by_group(f("L0_attn_bk"))[:, None], "wv": wv, "wo": f("L0_attn_Wo"),
        "wg": f("L0_ffn_Wg").T, "bg": f("L0_ffn_bg")[None, :], "wgu": wgu, "wd": f("L0_ffn_Wd"), "bdo": bdo,
        "ident": np.eye(P, dtype=np.float32), 
        "iota": np.tile(np.arange(NEXP, dtype=np.float32), (P, 1)),
    }
    arrays = {n: np.ascontiguousarray(a) for n, a in arrays.items()}
    nc = bacc.Bacc("TRN2", target_bir_lowering=False, num_devices=1)
    args = [nc.dram_tensor(f"in_{n}", a.shape, F32, kind="ExternalInput").ap() for n, a in arrays.items()]
    out = nc.dram_tensor("out", (B, S, D), F32, kind="ExternalOutput").ap()
    moe_attention_kernel(nc, *args, out)
    r = run_bass_kernel_spmd(nc, [{f"in_{n}": a for n, a in arrays.items()}], core_ids=[0])
    return r.results[0]["out"]
```

```python
from contextlib import ExitStack

import concourse.bass as bass
from concourse import mybir

P = 128
B, S, D = 2, 1024, 128
HEADS, DH, LATENT = 16, 8, 32
NEXP = 16
LIMIT, ALPHA, EPS = 7.0, 1.702, 1e-5
SCALE = float(DH) ** -0.5

TILES = B * S // P
CHUNKS = B * S // 512
PER_CHUNK = 4
HG = 4
NG = HEADS // HG
PG = B * NG
KB = S // P
PARTS = 3
PROD = PARTS * PARTS * DH
ROWS = PROD + PARTS
LEAD = 12
STEPS = 4 * KB
TURNS = PG // 2
BLOCKS = 48
GB = 4
GROUPS = BLOCKS // GB
WSLOTS = 4
RING = 3

ALU = mybir.AluOpType
ACT = mybir.ActivationFunctionType
AX_X = mybir.AxisListType.X
F32 = mybir.dt.float32
BF16 = mybir.dt.bfloat16
U32 = mybir.dt.uint32
I32 = mybir.dt.int32


def has_max(s, last):
    return not last or s + LEAD < STEPS


def has_max_turn(s, last):
    return s % KB == 5 and has_max(s - 2, last)


def has_value_turn(s):
    return s % KB == 2 and s >= KB


def jobs_before(s, start, last):
    return sum(4 * has_max(i, last) + has_max_turn(i, last) + has_value_turn(i) + (last and i in PROJECT) + (last and i - 1 in PROJECT)
               for i in range(start, s))


HEAD = 5
PROJECT = {20: (0, 0), 23: (0, 1), 29: (1, 0)}
TURN_OF_FIRST = 4 * KB + 2
AHEAD_JOBS = 4 * LEAD + 1
BEFORE_JOBS = AHEAD_JOBS + jobs_before(HEAD, 0, False)
TURN_JOBS = jobs_before(STEPS + HEAD, HEAD, False)


def moe_attention_kernel(nc, x, wq, bq, wl, bl, wk, bk, wv, wo, wg, bg, wexp, bdo, ident, iota, before, out):
    q_parts = nc.dram_tensor("q_parts", (PG, PARTS, DH * HG, S), BF16, kind="Internal").ap()
    k_parts = nc.dram_tensor("k_parts", (PG, PARTS, DH * HG, S), BF16, kind="Internal").ap()
    max_rows = nc.dram_tensor("max_rows", (2, PARTS * HG * 4, P), BF16, kind="Internal").ap()
    x_table = nc.dram_tensor("x_table", (BLOCKS * P, D), F32, kind="Internal").ap()
    moe_table = nc.dram_tensor("moe_table", (BLOCKS * P, D), F32, kind="Internal").ap()

    with ExitStack() as ctx:
        def sb(name, shape, dt=F32):
            return ctx.enter_context(nc.sbuf_tensor(name, shape, dt))

        def sem(name):
            return ctx.enter_context(nc.semaphore(name))

        id_f = sb("id_f", [P, P])
        id_b = sb("id_b", [P, P], BF16)
        iota_b = sb("iota_b", [P, BLOCKS])
        before_f = sb("before_f", [P, P])
        before_b = sb("before_b", [P, P], BF16)
        ones_b = sb("ones_b", [P, P], BF16)
        wq_sb = sb("wq_sb", [P, D])
        wl_sb = sb("wl_sb", [P, LATENT])
        wk_sb = sb("wk_sb", [LATENT, D])
        wv_sb = sb("wv_sb", [LATENT + 1, D])
        wo_sb = sb("wo_sb", [P, D])
        wg_sb = sb("wg_sb", [P, NEXP])
        bg_sb = sb("bg_sb", [P, NEXP])
        bq_sb = sb("bq_sb", [P, 1])
        bl_sb = sb("bl_sb", [LATENT, 1])
        bk_sb = sb("bk_sb", [P, 1])
        bdo_sb = sb("bdo_sb", [33, D])
        zeros = sb("zeros", [P, P])
        unused = sb("unused", [1, 2])
        y = sb("y", [P, TILES, D])
        xn = sb("xn", [P, TILES, D])
        xnT = sb("xnT", [P, B * S])
        stats = sb("stats", [P, TILES, 6])
        mv = sb("mv", [P, TILES, 2])
        rs = sb("rs", [P, 4, TILES])
        latT = sb("latT", [LATENT + 1, B * S])
        qf = sb("qf", [P, CHUNKS, 512])
        kf = sb("kf", [P, CHUNKS, 512])
        rq = sb("rq", [P, 512])
        rk = sb("rk", [P, 512])
        q3 = sb("q3", [P, CHUNKS, PARTS, 512], BF16)
        k3 = sb("k3", [P, CHUNKS, PARTS, 512], BF16)
        v_all = sb("v_all", [P, PG, KB, HG * DH])
        logits = sb("logits", [P, TILES, NEXP])
        top_v = sb("top_v", [P, TILES, 8])
        top_i = sb("top_i", [P, TILES, 8], U32)
        top_f = sb("top_f", [P, TILES, 2])
        tw = sb("tw", [P, 4, TILES])
        hot1 = sb("hot1", [P, TILES, NEXP])
        hot2 = sb("hot2", [P, TILES, NEXP])
        cw = sb("cw", [P, TILES, NEXP])
        cwT = sb("cwT", [33, B * S])
        both = sb("both", [P, TILES, NEXP], BF16)
        full = sb("full", [P, NEXP])
        over = sb("over", [P, NEXP, NEXP])
        blocks_of = sb("blocks_of", [P, NEXP])
        lower = sb("lower", [P, NEXP, NEXP])
        first_block = sb("first_block", [P, NEXP])
        first_row = sb("first_row", [P, NEXP])
        end_block = sb("end_block", [P, NEXP])
        place = sb("place", [P, TILES, NEXP])
        place_k = sb("place_k", [P, 2, TILES, NEXP])
        place_f = sb("place_f", [P, 2, TILES])
        place_u = sb("place_u", [P, 2, TILES], U32)
        ended = sb("ended", [1, BLOCKS, NEXP])
        expert_f = sb("expert_f", [1, BLOCKS])
        expert_i = sb("expert_i", [1, BLOCKS], I32)
        w_blk = sb("w_blk", [P, WSLOTS * GB, 3 * P + 2])
        q_rows = [sb(f"q_rows{i}", [ROWS, HG, S], BF16) for i in range(2)]
        k_rows = [sb(f"k_rows{i}", [ROWS, HG, S], BF16) for i in range(2)]
        v_pad = sb("v_pad", [P, 2, KB, HG, 32])
        probs = sb("probs", [P, 4, 2, 512])
        up = qf
        gate = kf[:, 0:2, :]
        th = kf[:, 2:4, :]
        x_rows = probs[:, 0:2, :, :].rearrange("p a b n -> p (a b) n")
        xT_blk = probs[:, 2, :, :]
        res = probs[:, 3, :, :]
        half_max = sb("half_max", [P, 2, 16, 2])
        neg_max = sb("neg_max", [P, 2, 16])
        max_rest = sb("max_rest", [P, 16])
        max3_pad = sb("max3_pad", [P, 2, P], BF16)
        max3 = max3_pad[:, :, 0:PARTS * 16].rearrange("p u (a r) -> p u a r", a=PARTS)
        maxT = sb("maxT", [PARTS * 16, 2, P], BF16)
        pv_sb = sb("pv_sb", [P, 2, 512])
        sum_inv = sb("sum_inv", [P, 4, HG])
        attn = sb("attn", [P, TILES, NG, HG * DH])
        attnT = rq

        banks = ctx.enter_context(nc.psum_tensor("banks", [P, 8, 512], F32))

        s_x = [sem(f"s_x{c}") for c in range(CHUNKS)]
        s_id = sem("s_id")
        s_w1 = sem("s_w1")
        s_w2 = sem("s_w2")
        s_dve = sem("s_dve")
        s_pool = sem("s_pool")
        s_var = sem("s_var")
        s_sqrt = sem("s_sqrt")
        s_xn = sem("s_xn")
        s_xt_ps = sem("s_xt_ps")
        s_xnT = sem("s_xnT")
        s_idb = sem("s_idb")
        s_rows1 = sem("s_rows1")
        s_lg = sem("s_lg")
        s_lg_sb = sem("s_lg_sb")
        s_lat_ps = sem("s_lat_ps")
        s_lat = sem("s_lat")
        s_q_ps = sem("s_q_ps")
        s_q = sem("s_q")
        s_k_ps = sem("s_k_ps")
        s_k = sem("s_k")
        s_v_ps = sem("s_v_ps")
        s_v = sem("s_v")
        s_q3 = sem("s_q3")
        s_k3 = [sem(f"s_k3_{b}") for b in range(B)]
        s_q3_out = [sem(f"s_q3_out{b}") for b in range(B)]
        s_k3_out = [sem(f"s_k3_out{b}") for b in range(B)]
        s_gap = sem("s_gap")
        s_egap = sem("s_egap")
        s_cw = sem("s_cw")
        s_cwT_ps = sem("s_cwT_ps")
        s_cwT = sem("s_cwT")
        s_bias_ps = sem("s_bias_ps")
        s_y = sem("s_y")
        s_zero = sem("s_zero")
        s_cleared = sem("s_cleared")
        s_tri = sem("s_tri")
        s_both = sem("s_both")
        s_rank = sem("s_rank")
        s_place = sem("s_place")
        s_expert = sem("s_expert")
        s_scattered = sem("s_scattered")
        s_wblk = [sem(f"s_wblk{i}") for i in range(WSLOTS)]
        s_xrows = [sem(f"s_xrows{i}") for i in range(4)]
        s_xfirst = [sem(f"s_xfirst{i}") for i in range(4)]
        s_xT_ps = sem("s_xT_ps")
        s_xT = sem("s_xT")
        s_gate_ps = sem("s_gate_ps")
        s_up_ps = sem("s_up_ps")
        s_up_in = sem("s_up_in")
        s_gate = sem("s_gate")
        s_up = sem("s_up")
        s_th = sem("s_th")
        s_glu = sem("s_glu")
        s_gated = sem("s_gated")
        s_down = sem("s_down")
        s_res = sem("s_res")
        s_res_out = [sem(f"s_res_out{i}") for i in range(2)]
        s_back = [sem(f"s_back{i}") for i in range(4)]
        s_moe = sem("s_moe")
        s_krow1 = sem("s_krow1")
        s_qk = [sem(f"s_qk{i}") for i in range(2)]
        s_vz = sem("s_vz")
        s_vpad = sem("s_vpad")
        ring_full = sem("ring_full")
        ring_free = sem("ring_free")
        s_negmax = sem("s_negmax")
        s_max3 = sem("s_max3")
        s_maxout = sem("s_maxout")
        s_maxin = [sem(f"s_maxin{i}") for i in range(2)]
        s_scores = sem("s_scores")
        s_exp = sem("s_exp")
        s_pv = sem("s_pv")
        s_pv_sb = sem("s_pv_sb")
        s_inv = sem("s_inv")
        s_out = sem("s_out")

        def late_step(k):
            return KB + k // 4, k % 4, 4 * KB + k + (k >= 2)

        QK_DMAS = 2 * PARTS

        def turn_base(turn):
            return BEFORE_JOBS + TURN_JOBS * turn

        LAT_BANK, Q_BANK, K_BANK, V_BANK = (5, 6, 7, 0), (1, 2, 1, 2), (3, 5, 3, 5), (6, 7, 6, 7)

        block = ctx.enter_context(nc.Block())

        @block.sync
        def _(sp):
            xv = x.rearrange("b (t p) d -> p (b t) d", p=P)
            ov = out.rearrange("b (t p) d -> p (b t) d", p=P)
            for c in range(CHUNKS):
                sp.dma_start(y[:, 4 * c:4 * c + 4, :], xv[:, 4 * c:4 * c + 4, :]).then_inc(s_x[c], 16)

            for dst, src in ((wk_sb, wk), (bk_sb, bk), (wv_sb, wv), (iota_b, iota), (before_f, before), (bdo_sb, bdo), (wo_sb, wo)):
                sp.dma_start(dst[:], src).then_inc(s_w2, 16)
            sp.wait_ge(s_zero, 1)
            sp.dma_start(x_table.rearrange("(n p) d -> p n d", p=P), zeros[:, None, :].to_broadcast([P, BLOCKS, D])).then_inc(s_cleared, 16)

            def experts_of(i, n):
                b = GB * (WSLOTS * i + n)
                return [sp.value_load(expert_i[0:1, b + q:b + q + 1] if isinstance(i, int) else expert_i[0:1, bass.ds(b + q, 1)],
                                      min_val=0, max_val=NEXP - 1) for q in range(GB)]

            def load_weights(n, experts):
                for q, e in enumerate(experts):
                    sp.dma_start(w_blk[:, GB * n + q, :], wexp[bass.ds(e, 1), :, :].rearrange("o p n -> (o p) n")).then_inc(s_wblk[n], 16)

            def load_group(g, slot):
                for a in range(PARTS):
                    rows = slice(a * PARTS * DH, (a + 1) * PARTS * DH)
                    part = k_parts[bass.ds(g, 1), a, :, :].rearrange("o (d j) t -> (o d) (j t)", j=HG)
                    sp.dma_start(k_rows[slot][rows, :, :].rearrange("r j t -> r (j t)"),
                                 part[None, :, :].to_broadcast([PARTS, DH, HG * S])).then_inc(s_qk[slot], 16)
                    sp.dma_start(q_rows[slot][rows, :, :].rearrange("r j t -> r (j t)"),
                                 q_parts[bass.ds(g, 1), :, :, :].rearrange("o c (d j) t -> (o c d) (j t)", j=HG)).then_inc(s_qk[slot], 16)

            def load_max(parity, slot, half, done):
                sp.dma_start(max_rows[parity], maxT[:, parity, :]).then_inc(s_maxout, 16)
                sp.wait_ge(s_maxout, 16 * done)
                sp.dma_start(q_rows[slot][PROD:ROWS, :, 512 * half:512 * half + 512],
                             max_rows[parity].rearrange("(a j q) t -> a j (q t)", a=PARTS, j=HG)).then_inc(s_maxin[parity], 16)

            def store_parts(c, parts, ready, dst, done):
                sp.wait_ge(ready, c + 1 if ready is s_q3 else c % 2 + 1)
                for g in range(NG):
                    t0 = 512 * (c % 2)
                    sp.dma_start(dst[NG * (c // 2) + g, :, :, t0:t0 + 512].rearrange("a r t -> r a t"),
                                 parts[32 * g:32 * g + 32, c, :, :]).then_inc(done, 16)

            def store_pair(b):
                for c in (2 * b, 2 * b + 1):
                    store_parts(c, q3, s_q3, q_parts, s_q3_out[b])
                for c in (2 * b, 2 * b + 1):
                    store_parts(c, k3, s_k3[b], k_parts, s_k3_out[b])

            store_pair(0)
            sp.wait_ge(s_q3_out[0], 16 * 2 * NG)
            sp.wait_ge(s_k3_out[0], 16 * 2 * NG)
            sp.wait_ge(s_krow1, 2)
            load_group(0, 0)
            load_group(1, 1)
            sp.wait_ge(s_expert, 1)
            for n in range(WSLOTS):
                load_weights(n, experts_of(0, n))
            store_pair(1)

            later = [experts_of(i, n) for i in range(1, GROUPS // WSLOTS) for n in range(WSLOTS)]
            sp.wait_ge(ring_free, TURN_OF_FIRST + 1)
            load_max(0, 0, 0, 1)
            for i in range(1, GROUPS // WSLOTS):
                for n in range(WSLOTS):
                    sp.wait_ge(s_down, WSLOTS * (i - 1) + n + 1 + WSLOTS)
                    load_weights(n, later[WSLOTS * (i - 1) + n])
            sp.wait_ge(s_q3_out[1], 16 * 2 * NG)
            sp.wait_ge(s_k3_out[1], 16 * 2 * NG)

            def turn(t, last):
                for s in range(HEAD, STEPS if last else STEPS + HEAD):
                    if s == STEPS // 2 and not last:
                        sp.wait_ge(s_scores, 2 * STEPS * t + STEPS)
                        load_group(2 * t + 2, 0)
                    if s == STEPS and not last:
                        sp.wait_ge(s_scores, 2 * STEPS * t + 2 * STEPS)
                        load_group(2 * t + 3, 1)
                    if has_max_turn(s, last):
                        unit = (s + LEAD - 2) // KB
                        sp.wait_ge(ring_free, turn_base(t) + jobs_before(s, HEAD, last) + 4 * has_max(s, last) + 1)
                        load_max(unit % 2, (unit // 2) % 2, unit % 2, 4 * t + unit + 1)
                    if last and s - 1 in PROJECT:
                        store(jobs_before(s + 1, HEAD, True), *PROJECT[s - 1])

            def store(jobs, b, half):
                sp.wait_ge(ring_free, turn_base(TURNS - 1) + jobs)
                t0 = 8 * b + 4 * half
                sp.dma_start(ov[:, t0:t0 + 4, :], y[:, t0:t0 + 4, :]).then_inc(s_out, 16)

            with sp.Fori(0, TURNS - 1) as t:
                turn(t, False)
            turn(TURNS - 1, True)
            store(jobs_before(STEPS, HEAD, True) + 3, 1, 1)
            sp.wait_ge(s_out, 16 * 2 * B)

        @block.gpsimd
        def _(pool):
            chain = [0]

            def link(ins):
                chain[0] += 1
                ins.then_inc(s_pool, 1)
                pool.wait_ge(s_pool, chain[0])

            nc.gpsimd.memset(zeros[:], 0.0).then_inc(s_zero, 1)
            pool.wait_ge(s_zero, 1)
            nc.gpsimd.memset(latT[LATENT:LATENT + 1, :], 1.0).then_inc(s_rows1, 1)
            pool.wait_ge(s_rows1, 1)
            link(nc.gpsimd.memset(cwT[:], 0.0))
            nc.gpsimd.memset(cwT[32:33, :], 1.0).then_inc(s_rows1, 1)
            pool.wait_ge(s_rows1, 2)
            nc.gpsimd.memset(unused[:, 0:1], 0.0).then_inc(s_down, WSLOTS)
            pool.wait_ge(s_down, WSLOTS)
            nc.gpsimd.memset(unused[:, 1:2], 0.0).then_inc(s_res, 1)
            pool.wait_ge(s_res, 1)
            link(nc.gpsimd.memset(ones_b[:], 1.0))
            pool.wait_ge(s_w2, 16 * 7)
            nc.gpsimd.tensor_copy(before_b[:], before_f[:]).then_inc(s_tri, 1)
            pool.wait_ge(s_tri, 1)
            for slot in range(2):
                nc.gpsimd.memset(k_rows[slot][64:ROWS, :, :], 1.0).then_inc(s_krow1, 1)
                pool.wait_ge(s_krow1, slot + 1)
            link(nc.gpsimd.memset(v_pad[:], 0.0))
            link(nc.gpsimd.memset(v_pad[:, :, :, :, DH:DH + 1], 1.0))
            link(nc.gpsimd.memset(max3_pad[:], 0.0))

            for c in range(2):
                pool.wait_ge(s_k, c + 1)
                link(nc.gpsimd.tensor_tensor(rk[:], kf[:, c, :], k3[:, c, 0, :], ALU.subtract))
                link(nc.gpsimd.tensor_tensor(k3[:, c, 1, :], rk[:], zeros[:, 0:1].to_broadcast([P, 512]), ALU.add))
                nc.gpsimd.tensor_tensor(k3[:, c, 2, :], rk[:], k3[:, c, 1, :], ALU.subtract).then_inc(s_k3[0], 1)
                pool.wait_ge(s_k3[0], c + 1)

            def fill_v(g, slot):
                pool.wait_ge(s_v, CHUNKS)
                nc.gpsimd.tensor_copy(
                    v_pad[:, slot, :, :, 0:DH],
                    v_all[:, bass.ds(g, 1), :, :].rearrange("p o k (j d) -> p (o k) j d", d=DH)).then_inc(s_vpad, 1)

            pool.wait_ge(s_place, 1)
            pool.wait_ge(s_cleared, 16)
            for k in range(2):
                for t in range(TILES):
                    pool.indirect_dma_start(x_table, bass.IndirectOffsetOnAxis(place_u[:, k, t:t + 1], 0), xn[:, t, :], None).then_inc(s_scattered, 16)
            pool.wait_ge(s_scattered, 16 * 2 * TILES)

            by_group = x_table.rearrange("(m q p) d -> m p q d", q=GB, p=P)
            res_by_group = moe_table.rearrange("(m q p) d -> m p q d", q=GB, p=P)

            def load_rows(m, n):
                pool.dma_start(x_rows[:, n, :].rearrange("p (q d) -> p q d", q=GB),
                               by_group[m]).then_inc(s_xrows[n], 16)

            def store_rows(m, n):
                pool.wait_ge(s_res, m + 1 + 1)
                pool.dma_start(res_by_group[m],
                               res[:, n, :].rearrange("p (q d) -> p q d", q=GB)).then_inc(s_res_out[n], 16)

            def split_max(parity, done):
                pool.wait_ge(s_negmax, done)
                base = 3 * (done - 1)
                nc.gpsimd.tensor_tensor(max3[:, parity, 0, :], neg_max[:, parity, :], zeros[:, 0:16], ALU.add).then_inc(s_vz, 1)
                pool.wait_ge(s_vz, base + 1)
                nc.gpsimd.tensor_tensor(max_rest[:], neg_max[:, parity, :], max3[:, parity, 0, :], ALU.subtract).then_inc(s_vz, 1)
                pool.wait_ge(s_vz, base + 2)
                nc.gpsimd.tensor_tensor(max3[:, parity, 1, :], max_rest[:], zeros[:, 0:16], ALU.add).then_inc(s_vz, 1)
                pool.wait_ge(s_vz, base + 3)
                nc.gpsimd.tensor_tensor(max3[:, parity, 2, :], max_rest[:], max3[:, parity, 1, :], ALU.subtract).then_inc(s_max3, 1)
                pool.wait_ge(s_max3, done)

            split_max(0, 1)
            fill_v(0, 0)
            fill_v(1, 1)
            for m in range(-3, GROUPS):
                if 4 <= m + 7 < GROUPS:
                    pool.wait_ge(s_xT_ps, m + 4)
                    load_rows(m + 7, (m + 7) % 4)
                if m >= 0:
                    store_rows(m, m % 2)

            back = (xn, xnT[:, :].rearrange("p (t d) -> p t d", d=D))

            def gather(k, t):
                pool.indirect_dma_start(back[k][:, t, :], None, moe_table,
                                        bass.IndirectOffsetOnAxis(place_u[:, k, t:t + 1], 0)).then_inc(s_back[t // 4], 16)

            def combine(h):
                pool.wait_ge(s_back[h], 16 * 8)
                ts = slice(4 * h, 4 * h + 4)
                for k in range(2):
                    nc.gpsimd.tensor_tensor(back[k][:, ts, :], back[k][:, ts, :],
                                            tw[:, 2 + k, ts].unsqueeze(2).to_broadcast([P, 4, D]), ALU.mult).then_inc(s_moe, 1)
                    pool.wait_ge(s_moe, 4 * h + 2 * k + 1)
                    nc.gpsimd.tensor_tensor(y[:, ts, :], y[:, ts, :], back[k][:, ts, :], ALU.add).then_inc(s_moe, 1)
                    pool.wait_ge(s_moe, 4 * h + 2 * k + 2)

            returns = []
            for h in range(CHUNKS):
                returns += [(gather, k, t) for t in range(4 * h, 4 * h + 4) for k in range(2)]
                if h:
                    returns.append((combine, h - 1))
            returns.append((combine, CHUNKS - 1))

            def turn(t, last):
                for s in range(HEAD, STEPS if last else STEPS + HEAD):
                    if has_max_turn(s, last):
                        unit = (s + LEAD - 2) // KB
                        split_max(unit % 2, 4 * t + unit + 1)
                    if s == 22 and not last:
                        pool.wait_ge(s_pv, STEPS * t + STEPS // 2)
                        fill_v(2 * t + 2, 0)
                    if s == STEPS + 2:
                        pool.wait_ge(s_pv, STEPS * t + STEPS)
                        fill_v(2 * t + 3, 1)
                    if last:
                        for what, *where in returns[3 * (s - HEAD) // 2:3 * (s - HEAD + 1) // 2]:
                            what(*where)

            with pool.Fori(0, TURNS - 1) as t:
                turn(t, False)
            for i in range(2):
                pool.wait_ge(s_res_out[i], 16 * (GROUPS // 2))
            turn(TURNS - 1, True)

        @block.scalar
        def _(act):
            act.dma_start(id_f[:], ident).then_inc(s_id, 16)
            for dst, src in ((wg_sb, wg), (wl_sb, wl), (bl_sb, bl), (wq_sb, wq), (bq_sb, bq)):
                act.dma_start(dst[:], src).then_inc(s_w1, 16)
            act.dma_start(bg_sb[:], bg.to_broadcast([P, NEXP])).then_inc(s_w1, 16)
            act.wait_ge(s_var, 1)
            nc.scalar.activation(rs[:, 1, :], rs[:, 0, :], ACT.Sqrt).then_inc(s_sqrt, 1)
            for c in range(CHUNKS):
                act.wait_ge(s_xt_ps, c + 1)
                nc.scalar.activation(xnT[:, 512 * c:512 * c + 512], banks[:, c, :], ACT.Copy).then_inc(s_xnT, 1)
            act.wait_ge(s_w1, 16 * 6)
            for c in range(CHUNKS):
                act.wait_ge(s_lat_ps, c + 1)
                nc.scalar.activation(latT[0:LATENT, 512 * c:512 * c + 512], banks[0:LATENT, LAT_BANK[c], :], ACT.Identity,
                                     bias=bl_sb[:, 0:1]).then_inc(s_lat, 1)
            def q_in(c):
                act.wait_ge(s_q_ps, c + 1)
                nc.scalar.activation(qf[:, c, :], banks[:, Q_BANK[c], :], ACT.Identity, bias=bq_sb[:, 0:1])
                nc.scalar.activation(q3[:, c, 0, :], banks[:, Q_BANK[c], :], ACT.Identity, bias=bq_sb[:, 0:1]).then_inc(s_q, 1)

            def k_in(c):
                act.wait_ge(s_k_ps, c + 1)
                nc.scalar.activation(kf[:, c, :], banks[:, K_BANK[c], :], ACT.Identity, bias=bk_sb[:, 0:1])
                nc.scalar.activation(k3[:, c, 0, :], banks[:, K_BANK[c], :], ACT.Identity, bias=bk_sb[:, 0:1]).then_inc(s_k, 1)

            act.wait_ge(s_w2, 16 * 7)
            for b in range(B):
                for part_in in (q_in, k_in):
                    part_in(2 * b)
                    part_in(2 * b + 1)
            act.wait_ge(s_gap, 1)
            nc.scalar.activation(tw[:, 1, :], tw[:, 0, :], ACT.Exp).then_inc(s_egap, 1)
            for c in range(CHUNKS):
                act.wait_ge(s_v_ps, c + 1)
                nc.scalar.activation(
                    v_all[:, NG * (c // 2):NG * (c // 2) + NG, 4 * (c % 2):4 * (c % 2) + 4, :],
                    banks[:, V_BANK[c], :].rearrange("p (k g n) -> p g k n", k=4, g=NG), ACT.Copy).then_inc(s_v, 1)
            act.wait_ge(s_rows1, 2)

            for c in range(CHUNKS):
                act.wait_ge(s_cwT_ps, c + 1)
                nc.scalar.activation(cwT[0:NEXP, 512 * c:512 * c + 512], banks[0:NEXP, 1 + c, :], ACT.Copy).then_inc(s_cwT, 1)
            def keep_pv(t, unit):
                act.wait_ge(s_pv, STEPS * t + KB * (unit + 1))
                nc.scalar.activation(pv_sb[:, unit % 2, :], banks[:, 4, :], ACT.Copy).then_inc(s_pv_sb, 1)

            def exponentials(t, s, pairs=(0, 1)):
                for pair in pairs:
                    n = 2 * s + pair
                    act.wait_ge(s_scores, 2 * STEPS * t + n + 1)
                    if isinstance(t, int) and t == 0 and n == 3:
                        for i in range(2):
                            act.wait_ge(s_res_out[i], 16 * (GROUPS // 2))
                    if s >= 2:
                        act.wait_ge(s_pv, STEPS * t + s - 1)
                    nc.scalar.activation(probs[:, n % 4, :, :], banks[:, 2 * pair:2 * pair + 2, :], ACT.Exp,
                                         scale=SCALE).then_inc(s_exp, 1)
                if s % KB == 0 and s > 0:
                    keep_pv(t, s // KB - 1)

            def turned_rows(i, n):
                act.wait_ge(s_xT_ps, 4 * i + n + 1)
                if n >= 2 or not (isinstance(i, int) and i == 0):
                    act.wait_ge(s_up_ps, 4 * i + n - 1)
                nc.scalar.activation(xT_blk[:, n % 2, :], banks[:, 0, :], ACT.Copy).then_inc(s_xT, 1)

            def up_in(i, n):
                act.wait_ge(s_up_ps, 4 * i + n + 1)
                act.wait_ge(s_down, 4 * i + n + 1)
                for q in range(GB):
                    last = nc.scalar.activation(up[:, n % 4, P * q:P * q + P], banks[:, 2 + n % 2, P * q:P * q + P], ACT.Identity,
                                                bias=w_blk[:, GB * (n % 4) + q, 2 * P + 1:2 * P + 2])
                last.then_inc(s_up_in, 1)

            def tanh_of(i, n):
                act.wait_ge(s_gate, 4 * i + n + 1)
                if n >= 2 or not (isinstance(i, int) and i == 0):
                    act.wait_ge(s_gated, 4 * i + n - 1)
                nc.scalar.activation(th[:, n % 2, :], gate[:, n % 2, :], ACT.Tanh, scale=ALPHA / 2).then_inc(s_th, 1)

            def result_in(i, n):
                act.wait_ge(s_down, 4 * i + n + 1 + WSLOTS)
                if n >= 2 or not isinstance(i, int) or i > 0:
                    act.wait_ge(s_res_out[n % 2], 16 * (2 * i + n // 2))
                nc.scalar.activation(res[:, n % 2, :], banks[:, 4, :], ACT.Copy, scale=0.5).then_inc(s_res, 1)

            act.wait_ge(s_scattered, 16 * 2 * TILES)
            for n in range(4):
                act.dma_start(x_rows[:, n, :].rearrange("p (q d) -> p q d", q=GB),
                              x_table.rearrange("(m q p) d -> m p q d", q=GB, p=P)[n]).then_inc(s_xfirst[n], 16)
            act.wait_ge(s_q3, CHUNKS)
            for b in range(B):
                act.wait_ge(s_k3[b], 2)
            for n in range(3):
                turned_rows(0, n)
                if n < 2:
                    up_in(0, n)
                    tanh_of(0, n)

            def pieces(i, last):
                for n in range(4):
                    if not last or n + 3 < 4:
                        turned_rows(i, n + 3)
                    if not last or n + 2 < 4:
                        up_in(i, n + 2)
                        tanh_of(i, n + 2)
                    if last and n >= 2:
                        exponentials(0, 0, (n - 2,))
                    result_in(i, n)

            pieces(0, False)
            with act.Fori(1, GROUPS // 4 - 1) as i:
                pieces(i, False)
            pieces(GROUPS // 4 - 1, True)
            for s in range(1, HEAD):
                exponentials(0, s)
            with act.Fori(0, TURNS - 1) as t:
                for s in range(HEAD, STEPS + HEAD):
                    exponentials(t, s)
            for s in range(HEAD, STEPS):
                exponentials(TURNS - 1, s)
            keep_pv(TURNS - 1, 3)

        @block.vector
        def _(dve):
            chain = [0]

            def link(ins):
                chain[0] += 1
                ins.then_inc(s_dve, 1)
                dve.wait_ge(s_dve, chain[0])

            for c in range(CHUNKS):
                dve.wait_ge(s_x[c], 16)
                for t in range(4 * c, 4 * c + 4):
                    last = nc.vector.bn_stats(stats[:, t, :], y[:, t, :])
            link(last)
            for t in range(TILES):
                last = nc.vector.bn_aggr(mv[:, t, :], stats[:, t, :])
            link(last)
            nc.vector.tensor_scalar(rs[:, 0, :], mv[:, :, 1], EPS, None, ALU.add).then_inc(s_var, 1)
            dve.wait_ge(s_sqrt, 1)
            link(nc.vector.reciprocal(rs[:, 2, :], rs[:, 1, :]))
            link(nc.vector.tensor_tensor(rs[:, 3, :], rs[:, 2, :], rs[:, 2, :], ALU.mult))
            link(nc.vector.tensor_tensor(rs[:, 1, :], rs[:, 3, :], rs[:, 0, :], ALU.mult))
            link(nc.vector.tensor_scalar(rs[:, 3, :], rs[:, 1, :], -0.5, 1.5, ALU.mult, ALU.add))
            link(nc.vector.tensor_tensor(rs[:, 1, :], rs[:, 2, :], rs[:, 3, :], ALU.mult))
            for t in range(TILES):
                nc.vector.tensor_scalar(xn[:, t, :], y[:, t, :], mv[:, t, 0:1], rs[:, 1, t:t + 1],
                                        ALU.subtract, ALU.mult).then_inc(s_xn, 1)
            dve.wait_ge(s_id, 16)
            nc.vector.tensor_copy(id_b[:], id_f[:]).then_inc(s_idb, 1)
            dve.wait_ge(s_w2, 16 * 7)
            iota_e = iota_b[:, 0:NEXP]
            nc.vector.tensor_tensor(lower[:, :, :], iota_e.unsqueeze(2).to_broadcast([P, NEXP, NEXP]),
                                    iota_e[:, None, :].to_broadcast([P, NEXP, NEXP]), ALU.is_gt).then_inc(s_dve, 1)
            chain[0] += 1
            dve.wait_ge(s_lg, CHUNKS)
            dve.wait_ge(s_w1, 16 * 6)
            link(nc.vector.tensor_tensor(logits[:, :, :], banks[:, 4, 0:TILES * NEXP].rearrange("p (t e) -> p t e", e=NEXP),
                                         bg_sb[:, None, :].to_broadcast([P, TILES, NEXP]), ALU.add))
            for t in range(TILES):
                last = nc.vector.max(top_v[:, t, :], logits[:, t, :])
            link(last)
            for t in range(TILES):
                last = nc.vector.max_index(top_i[:, t, :], top_v[:, t, :], logits[:, t, :])
            link(last)
            link(nc.vector.tensor_copy(top_f[:, :, :], top_i[:, :, 0:2]))
            experts = iota_e[:, None, :].to_broadcast([P, TILES, NEXP])
            for k, hot in ((0, hot1), (1, hot2)):
                link(nc.vector.tensor_tensor(hot[:, :, :], top_f[:, :, k:k + 1].to_broadcast([P, TILES, NEXP]), experts, ALU.is_equal))
            nc.vector.tensor_tensor(both[:, :, :], hot1[:, :, :], hot2[:, :, :], ALU.add).then_inc(s_both, 1)
            nc.vector.tensor_tensor(tw[:, 0, :], top_v[:, :, 1], top_v[:, :, 0], ALU.subtract).then_inc(s_gap, 1)

            def split_q(c):
                dve.wait_ge(s_q, c + 1)
                link(nc.vector.tensor_tensor(rq[:], qf[:, c, :], q3[:, c, 0, :], ALU.subtract))
                link(nc.vector.tensor_copy(q3[:, c, 1, :], rq[:]))
                nc.vector.tensor_tensor(q3[:, c, 2, :], rq[:], q3[:, c, 1, :], ALU.subtract).then_inc(s_q3, 1)
                dve.wait_ge(s_q3, c + 1)

            split_q(0)
            split_q(1)

            dve.wait_ge(s_rank, 1)
            counts = banks[:, 0, 0:(TILES + 1) * NEXP].rearrange("p (t e) -> p t e", e=NEXP)
            link(nc.vector.tensor_scalar(full[:], counts[:, TILES, :], 1.0 / P, None, ALU.mult))
            link(nc.vector.tensor_tensor(over[:, :, :], full[:].unsqueeze(2).to_broadcast([P, NEXP, NEXP]),
                                         iota_e[:, None, :].to_broadcast([P, NEXP, NEXP]), ALU.is_gt))
            link(nc.vector.tensor_reduce(blocks_of[:], over[:, :, :], AX_X, ALU.add))
            link(nc.vector.tensor_tensor(over[:, :, :], lower[:, :, :], blocks_of[:, None, :].to_broadcast([P, NEXP, NEXP]), ALU.mult))
            link(nc.vector.tensor_reduce(first_block[:], over[:, :, :], AX_X, ALU.add))
            link(nc.vector.tensor_scalar(first_row[:], first_block[:], float(P), None, ALU.mult))
            link(nc.vector.tensor_tensor(place[:, :, :], counts[:, 0:TILES, :], first_row[:, None, :].to_broadcast([P, TILES, NEXP]), ALU.add))
            for k, hot in ((0, hot1), (1, hot2)):
                link(nc.vector.tensor_tensor(place_k[:, k, :, :], hot[:, :, :], place[:, :, :], ALU.mult))
            link(nc.vector.tensor_reduce(place_f[:, :, :].rearrange("p k t -> p (k t)"),
                                         place_k[:, :, :, :].rearrange("p k t e -> p (k t) e"), AX_X, ALU.add))
            nc.vector.tensor_copy(place_u[:, :, :], place_f[:, :, :]).then_inc(s_place, 1)
            link(nc.vector.tensor_tensor(end_block[:], first_block[:], blocks_of[:], ALU.add))
            link(nc.vector.tensor_tensor(ended[:, :, :], iota_b[0:1, :].unsqueeze(2).to_broadcast([1, BLOCKS, NEXP]),
                                         end_block[0:1, None, :].to_broadcast([1, BLOCKS, NEXP]), ALU.is_ge))
            link(nc.vector.tensor_reduce(expert_f[:], ended[:, :, :], AX_X, ALU.add))
            nc.vector.tensor_scalar(expert_i[:], expert_f[:], float(NEXP - 1), None, ALU.min).then_inc(s_expert, 1)

            split_q(2)
            split_q(3)
            dve.wait_ge(s_egap, 1)
            link(nc.vector.tensor_scalar(tw[:, 0, :], tw[:, 1, :], 1.0, None, ALU.add))
            link(nc.vector.reciprocal(tw[:, 2, :], tw[:, 0, :]))
            link(nc.vector.tensor_tensor(tw[:, 3, :], tw[:, 1, :], tw[:, 2, :], ALU.mult))
            for k, hot in ((0, hot1), (1, hot2)):
                link(nc.vector.tensor_tensor(hot[:, :, :], hot[:, :, :],
                                             tw[:, 2 + k, :].unsqueeze(2).to_broadcast([P, TILES, NEXP]), ALU.mult))
            nc.vector.tensor_tensor(cw[:, :, :], hot1[:, :, :], hot2[:, :, :], ALU.add).then_inc(s_cw, 1)
            for c in (2, 3):
                dve.wait_ge(s_k, c + 1)
                link(nc.vector.tensor_tensor(rq[:], kf[:, c, :], k3[:, c, 0, :], ALU.subtract))
                link(nc.vector.tensor_copy(k3[:, c, 1, :], rq[:]))
                nc.vector.tensor_tensor(k3[:, c, 2, :], rq[:], k3[:, c, 1, :], ALU.subtract).then_inc(s_k3[1], 1)
                dve.wait_ge(s_k3[1], c - 1)
            def max_job(job, base, ahead, m):
                unit = (ahead // KB) % 2
                row, half = divmod(4 * (ahead % KB) + m, 2)
                dve.wait_ge(ring_full, base + job + 1)
                nc.vector.tensor_reduce(half_max[:, unit, row, half:half + 1], banks[:, 5 + job % RING, :],
                                        AX_X, ALU.max).then_inc(ring_free, 1)
                if ahead % KB == KB - 1 and m == 3:
                    dve.wait_ge(ring_free, base + job + 1)
                    nc.vector.tensor_reduce(neg_max[:, unit, :], half_max[:, unit, :, :], AX_X, ALU.max,
                                            negate=True).then_inc(s_negmax, 1)

            def max_jobs(base, job, ahead):
                for m in range(4):
                    max_job(job + m, base, ahead, m)

            def maxima_turned(base, job, unit):
                dve.wait_ge(ring_full, base + job + 1)
                nc.vector.tensor_copy(maxT[:, unit % 2, :],
                                      banks[0:PARTS * 16, 5 + job % RING, 0:P // 2].bitcast(BF16)).then_inc(ring_free, 1)

            def normalise(base, job, t, unit):
                rows = banks[:, 5 + job % RING, :].rearrange("p (q j m) -> p q j m", q=4, j=HG)
                dve.wait_ge(ring_full, base + job + 1)
                nc.vector.reciprocal(sum_inv[:, :, :], rows[:, :, :, DH]).then_inc(s_inv, 1)
                dve.wait_ge(s_inv, 4 * t + unit + 1)
                nc.vector.tensor_tensor(
                    attn[:, bass.ds((t // 2) * 8 + (unit % 2) * 4, 4), bass.ds((t % 2) * 2 + unit // 2, 1), :].rearrange(
                        "p q o (j d) -> p q (o j) d", d=DH),
                    rows[:, :, :, 0:DH], sum_inv[:, :, :].unsqueeze(3).to_broadcast([P, 4, HG, DH]),
                    ALU.mult).then_inc(ring_free, 1)

            def rows_turned(base, job):
                dve.wait_ge(ring_full, base + job + 1)
                nc.vector.tensor_copy(attnT[:, :], banks[:, 5 + job % RING, :]).then_inc(ring_free, 1)

            def add_out(base, job, b, half):
                dve.wait_ge(ring_full, base + job + 1)
                t0 = 8 * b + 4 * half
                yc = y[:, t0:t0 + 4, :].rearrange("p t d -> p (t d)")
                dve.wait_ge(s_moe, 4 * (2 * b + half) + 4)
                nc.vector.tensor_tensor(yc, yc, banks[:, 5 + job % RING, :], ALU.add).then_inc(ring_free, 1)

            def add_bias(c):
                dve.wait_ge(s_bias_ps, c + 1)
                yc = y[:, 4 * c:4 * c + 4, :].rearrange("p t d -> p (t d)")
                nc.vector.tensor_tensor(yc, yc, banks[:, 1 + c, :], ALU.add).then_inc(s_y, 1)

            add_bias(0)
            add_bias(1)
            for m in range(KB):
                max_jobs(0, 4 * m, m)
                if m in (1, 2):
                    add_bias(m + 1)
            def late_job(k):
                ahead, m, job = late_step(k)
                max_job(job, 0, ahead, m)

            def gate_of(i, n):
                dve.wait_ge(s_gate_ps, 4 * i + n + 1)
                if n >= 2 or not (isinstance(i, int) and i == 0):
                    dve.wait_ge(s_glu, 4 * i + n - 1)
                for q in range(GB):
                    last = nc.vector.tensor_scalar(gate[:, n % 2, P * q:P * q + P], banks[:, 1, P * q:P * q + P],
                                                   w_blk[:, GB * (n % 4) + q, 2 * P:2 * P + 1], LIMIT, ALU.add, ALU.min)
                last.then_inc(s_gate, 1)

            def up_of(i, n):
                u = up[:, n % 4, :]
                dve.wait_ge(s_up_in, 4 * i + n + 1)
                nc.vector.tensor_scalar(u, u, -LIMIT, LIMIT, ALU.max, ALU.min).then_inc(s_up, 1)

            def gated_of(i, n):
                dve.wait_ge(s_th, 4 * i + n + 1)
                nc.vector.scalar_tensor_tensor(out=th[:, n % 2, :], in0=th[:, n % 2, :], scalar=1.0,
                                               in1=gate[:, n % 2, :], op0=ALU.add, op1=ALU.mult).then_inc(s_glu, 1)
                dve.wait_ge(s_up, 4 * i + n + 1)
                dve.wait_ge(s_glu, 4 * i + n + 1)
                nc.vector.scalar_tensor_tensor(out=up[:, n % 4, :], in0=up[:, n % 4, :], scalar=1.0,
                                               in1=th[:, n % 2, :], op0=ALU.add, op1=ALU.mult).then_inc(s_gated, 1)

            dve.wait_ge(s_k3[0], 2)
            late_job(0)
            late_job(1)
            gate_of(0, 0)
            maxima_turned(0, TURN_OF_FIRST, 0)
            late_job(2)
            late_job(3)
            up_of(0, 0)
            gate_of(0, 1)
            late_job(4)
            late_job(5)
            gated_of(0, 0)
            up_of(0, 1)

            def pieces(i, last, late=0, first_late=0):
                for n in range(4):
                    if not last or n + 2 < 4:
                        gate_of(i, n + 2)
                    if n < late:
                        late_job(first_late + 2 * n)
                    if not last or n + 1 < 4:
                        gated_of(i, n + 1)
                    if n < late:
                        late_job(first_late + 2 * n + 1)
                    if not last or n + 2 < 4:
                        up_of(i, n + 2)

            pieces(0, False, 4, 6)
            with dve.Fori(1, GROUPS // 4 - 1) as i:
                pieces(i, False)
            pieces(GROUPS // 4 - 1, True, 1, 14)

            def step(base, job, t, s, last):
                if has_max(s, last):
                    max_jobs(base, job, s + LEAD)
                    job += 4
                if has_max_turn(s, last):
                    maxima_turned(base, job, (s + LEAD - 2) // KB)
                    job += 1
                if has_value_turn(s):
                    normalise(base, job, t, s // KB - 1)
                    job += 1
                if last and s in PROJECT:
                    rows_turned(base, job)
                if last and s - 1 in PROJECT:
                    add_out(base, job, *PROJECT[s - 1])

            for s in range(HEAD):
                step(0, AHEAD_JOBS + jobs_before(s, 0, False), 0, s, False)
            with dve.Fori(0, TURNS - 1) as t:
                for s in range(HEAD, STEPS + HEAD):
                    step(turn_base(t), jobs_before(s, HEAD, False), t, s, False)
            base = turn_base(TURNS - 1)
            for s in range(HEAD, STEPS):
                step(base, jobs_before(s, HEAD, True), TURNS - 1, s, True)
            job = jobs_before(STEPS, HEAD, True)
            normalise(base, job, TURNS - 1, 3)
            rows_turned(base, job + 1)
            add_out(base, job + 2, 1, 1)

        @block.tensor
        def _(pe):
            pe.wait_ge(s_id, 16)
            def turn_tokens(c):
                pe.wait_ge(s_xn, 4 * c + 4)
                for t in range(4):
                    last = pe.transpose(banks[:, c, P * t:P * t + P], xn[:, 4 * c + t, :], id_f[:])
                last.then_inc(s_xt_ps, 1)

            def router(c):
                pe.wait_ge(s_xnT, c + 1)
                for t in range(4 * c, 4 * c + 4):
                    last = pe.matmul(banks[:, 4, NEXP * t:NEXP * t + NEXP], xnT[:, P * t:P * t + P], wg_sb[:], start=True, stop=True)
                last.then_inc(s_lg, 1)

            turn_tokens(0)
            turn_tokens(1)
            pe.wait_ge(s_w1, 16 * 6)
            router(0)
            turn_tokens(2)
            router(1)
            turn_tokens(3)
            router(2)
            router(3)
            for c in range(CHUNKS):
                pe.matmul(banks[0:LATENT, LAT_BANK[c], :], wl_sb[:], xnT[:, 512 * c:512 * c + 512],
                          start=True, stop=True).then_inc(s_lat_ps, 1)

            def project_q(c):
                if c >= 2:
                    pe.wait_ge(s_q, c - 1)
                pe.matmul(banks[:, Q_BANK[c], :], wq_sb[:], xnT[:, 512 * c:512 * c + 512], start=True, stop=True).then_inc(s_q_ps, 1)

            def project_k(c):
                if c >= 2:
                    pe.wait_ge(s_k, c - 1)
                pe.matmul(banks[:, K_BANK[c], :], wk_sb[:], latT[0:LATENT, 512 * c:512 * c + 512], start=True, stop=True).then_inc(s_k_ps, 1)

            project_q(0)
            project_q(1)
            pe.wait_ge(s_lat, CHUNKS)
            pe.wait_ge(s_w2, 16 * 7)
            pe.wait_ge(s_rows1, 2)
            project_k(0)
            project_k(1)
            pe.wait_ge(s_both, 1)
            pe.wait_ge(s_tri, 1)
            pe.matmul(banks[:, 0, 0:TILES * NEXP], before_b[:], both[:, :, :].rearrange("p t e -> p (t e)"),
                      start=True, stop=False, skip_group_check=True)
            for t in range(TILES):
                last = pe.matmul(banks[:, 0, (t + 1) * NEXP:(TILES + 1) * NEXP].rearrange("p (t e) -> p t e", e=NEXP), ones_b[:],
                                 both[:, t:t + 1, :].to_broadcast([P, TILES - t, NEXP]),
                                 start=False, stop=(t == TILES - 1), skip_group_check=True)
            last.then_inc(s_rank, 1)
            for c in (2, 3):
                project_q(c)
            for c in (2, 3):
                project_k(c)
            for c in range(CHUNKS):
                if c >= 2:
                    pe.wait_ge(s_v, c - 1)
                for t in range(4):
                    last = pe.matmul(banks[:, V_BANK[c], P * t:P * t + P], latT[:, 512 * c + P * t:512 * c + P * t + P], wv_sb[:],
                                     start=True, stop=True)
                last.then_inc(s_v_ps, 1)
            def ring_slot(base, job, first):
                if job >= RING:
                    pe.wait_ge(ring_free, base + job - RING + 1)
                elif not first:
                    pe.wait_ge(ring_free, base)
                return banks[:, 5 + job % RING, :]

            def max_job(base, job, ahead, m, first=False):
                unit = ahead // KB
                slot, half = (unit // 2) % 2, unit % 2
                row, keys = divmod(4 * (ahead % KB) + m, 2)
                j, qb = divmod(row, 4)
                bank = ring_slot(base, job + m, first)
                q0 = 512 * half + P * qb
                pe.matmul(bank, q_rows[slot][0:PROD, j, q0:q0 + P], k_rows[slot][0:PROD, j, 512 * keys:512 * keys + 512],
                          start=True, stop=True).then_inc(ring_full, 1)

            def turn_maxima(base, job, unit, done):
                pe.wait_ge(s_max3, done)
                bank = ring_slot(base, job, False)
                pe.transpose(bank[:, 0:P // 2].bitcast(BF16), max3_pad[:, unit % 2, :], id_b[:]).then_inc(ring_full, 1)

            def values(t, s):
                unit, kb = divmod(s, KB)
                slot = (unit // 2) % 2
                pe.wait_ge(s_exp, 2 * STEPS * t + 2 * s + 2)
                if kb == 0:
                    if unit > 0:
                        pe.wait_ge(s_pv_sb, 4 * t + unit)
                    pe.wait_ge(s_vpad, 2 * t + unit // 2 + 1)
                for j in range(HG):
                    mm = pe.matmul(banks[32 * j:32 * j + 32, 4, :], v_pad[:, slot, kb, j, :],
                                   probs[:, (2 * s + j // 2) % 4, j % 2, :], start=(kb == 0), stop=(kb == KB - 1))
                mm.then_inc(s_pv, 1)

            def turn_values(base, job, t, unit):
                pe.wait_ge(s_pv_sb, 4 * t + unit + 1)
                bank = ring_slot(base, job, False)
                for q in range(4):
                    mm = pe.transpose(bank[:, P * q:P * q + P], pv_sb[:, unit % 2, P * q:P * q + P], id_f[:])
                mm.then_inc(ring_full, 1)

            def turn_rows(base, job, b, half):
                pe.wait_ge(ring_free, base + job)
                bank = ring_slot(base, job, False)
                for q in range(4):
                    mm = pe.transpose(bank[:, P * q:P * q + P], attn[:, 8 * b + 4 * half + q, :, :].rearrange("p g n -> p (g n)"), id_f[:])
                mm.then_inc(ring_full, 1)

            def project(base, job):
                pe.wait_ge(ring_free, base + job)
                bank = ring_slot(base, job, False)
                for q in range(4):
                    mm = pe.matmul(bank[:, P * q:P * q + P], attnT[:, P * q:P * q + P], wo_sb[:], start=True, stop=True)
                mm.then_inc(ring_full, 1)

            def scores(t, s, pair):
                unit, kb = divmod(s, KB)
                slot, half = (unit // 2) % 2, unit % 2
                if kb == 0 and pair == 0:
                    pe.wait_ge(s_maxin[half], 16 * (2 * t + unit // 2 + 1))
                if s > 0:
                    pe.wait_ge(s_exp, 2 * STEPS * t + 2 * (s - 1) + pair + 1)
                for j in (2 * pair, 2 * pair + 1):
                    mm = pe.matmul(banks[:, j, :], k_rows[slot][0:ROWS, j, P * kb:P * kb + P],
                                   q_rows[slot][0:ROWS, j, 512 * half:512 * half + 512], start=True, stop=True)
                mm.then_inc(s_scores, 1)

            pe.wait_ge(s_cw, 1)
            pe.wait_ge(s_q, CHUNKS)
            pe.wait_ge(s_k, CHUNKS)
            for c in range(CHUNKS):
                for t in range(4):
                    last = pe.transpose(banks[0:NEXP, 1 + c, P * t:P * t + P], cw[:, 4 * c + t, :], id_f[:])
                last.then_inc(s_cwT_ps, 1)

            def bias(c):
                pe.wait_ge(s_cwT, c + 1)
                for t in range(4):
                    last = pe.matmul(banks[:, 1 + c, P * t:P * t + P], cwT[:, 512 * c + P * t:512 * c + P * t + P], bdo_sb[:],
                                     start=True, stop=True)
                last.then_inc(s_bias_ps, 1)

            bias(0)
            bias(1)
            pe.wait_ge(s_idb, 1)
            pe.wait_ge(s_v, CHUNKS)
            pe.wait_ge(s_qk[0], 16 * QK_DMAS)
            for m in range(KB):
                for k in range(4):
                    max_job(0, 4 * m, m, k, m == 0)
                if m < 2:
                    bias(m + 2)

            def late_job(k):
                ahead, m, job = late_step(k)
                max_job(0, job - m, ahead, m)

            def turn_rows_in(i, n):
                if isinstance(i, int) and i == 0 and n < 4:
                    pe.wait_ge(s_xfirst[n], 16)
                else:
                    pe.wait_ge(s_xrows[n % 4], 16 * (i + n // 4))
                if n >= 1 or not (isinstance(i, int) and i == 0):
                    pe.wait_ge(s_xT, 4 * i + n)
                for q in range(GB):
                    mm = pe.transpose(banks[:, 0, P * q:P * q + P], x_rows[:, n % 4, P * q:P * q + P], id_f[:])
                mm.then_inc(s_xT_ps, 1)

            def gate_up(i, n):
                pe.wait_ge(s_wblk[n % 4], 16 * GB * (i + n // 4) + 16 * GB)
                pe.wait_ge(s_xT, 4 * i + n + 1)
                if n >= 1 or not (isinstance(i, int) and i == 0):
                    pe.wait_ge(s_gate, 4 * i + n)
                for q in range(GB):
                    mm = pe.matmul(banks[:, 1, P * q:P * q + P], w_blk[:, GB * (n % 4) + q, 0:P],
                                   xT_blk[:, n % 2, P * q:P * q + P], start=True, stop=True)
                mm.then_inc(s_gate_ps, 1)
                if n >= 2 or not (isinstance(i, int) and i == 0):
                    pe.wait_ge(s_up_in, 4 * i + n - 1)
                for q in range(GB):
                    mm = pe.matmul(banks[:, 2 + n % 2, P * q:P * q + P], w_blk[:, GB * (n % 4) + q, P:2 * P],
                                   xT_blk[:, n % 2, P * q:P * q + P], start=True, stop=True)
                mm.then_inc(s_up_ps, 1)

            def down(i, n):
                pe.wait_ge(s_gated, 4 * i + n + 1)
                pe.wait_ge(s_res, 4 * i + n + 1)
                for q in range(GB):
                    mm = pe.matmul(banks[:, 4, P * q:P * q + P], up[:, n, P * q:P * q + P],
                                   w_blk[:, GB * n + q, 2 * P + 2:3 * P + 2], start=True, stop=True)
                mm.then_inc(s_down, 1)

            pe.wait_ge(s_y, CHUNKS)
            late_job(0)
            late_job(1)
            for n in range(3):
                turn_rows_in(0, n)
                if n < 2:
                    gate_up(0, n)
                if n == 0:
                    turn_maxima(0, TURN_OF_FIRST, 0, 1)
                if n < 2:
                    late_job(2 + 2 * n)
                    late_job(3 + 2 * n)

            def pieces(i, last, late=0, first_late=0):
                for n in range(4):
                    if not last or n + 3 < 4:
                        turn_rows_in(i, n + 3)
                    if n < late:
                        late_job(first_late + 2 * n)
                    if last and n >= 2:
                        pe.wait_ge((s_gate, s_up_in)[n - 2], GROUPS)
                        scores(0, 0, n - 2)
                    if not last or n + 2 < 4:
                        gate_up(i, n + 2)
                    if n < late:
                        late_job(first_late + 2 * n + 1)
                    down(i, n)

            pieces(0, False, 4, 6)
            with pe.Fori(1, GROUPS // 4 - 1) as i:
                pieces(i, False)
            pieces(GROUPS // 4 - 1, True, 1, 14)

            def step(base, job, t, s, last):
                if s == 4:
                    pe.wait_ge(s_qk[1], 16 * QK_DMAS)
                if s == 20 and not last:
                    pe.wait_ge(s_qk[0], 16 * QK_DMAS * (t + 2))
                if s == 36:
                    pe.wait_ge(s_qk[1], 16 * QK_DMAS * (t + 2))
                maxima = has_max(s, last)
                first = isinstance(t, int) and t == 0 and s == 0
                if not first:
                    scores(t, s, 0)
                if maxima:
                    max_job(base, job, s + LEAD, 0)
                if not first:
                    scores(t, s, 1)
                if maxima:
                    max_job(base, job, s + LEAD, 1)
                if first:
                    pe.wait_ge(s_res, GROUPS + 1)
                if s > 0:
                    values(t, s - 1)
                if maxima:
                    max_job(base, job, s + LEAD, 2)
                    max_job(base, job, s + LEAD, 3)
                    job += 4
                if has_max_turn(s, last):
                    unit = (s + LEAD - 2) // KB
                    turn_maxima(base, job, unit, 4 * t + unit + 1)
                    job += 1
                if has_value_turn(s):
                    turn_values(base, job, t, s // KB - 1)
                    job += 1
                if last and s in PROJECT:
                    turn_rows(base, job, *PROJECT[s])
                if last and s - 1 in PROJECT:
                    project(base, job)

            for s in range(HEAD):
                step(0, AHEAD_JOBS + jobs_before(s, 0, False), 0, s, False)
            with pe.Fori(0, TURNS - 1) as t:
                for s in range(HEAD, STEPS + HEAD):
                    step(turn_base(t), jobs_before(s, HEAD, False), t, s, False)
            base = turn_base(TURNS - 1)
            for s in range(HEAD, STEPS):
                step(base, jobs_before(s, HEAD, True), TURNS - 1, s, True)
            values(TURNS - 1, STEPS - 1)
            job = jobs_before(STEPS, HEAD, True)
            turn_values(base, job, TURNS - 1, 3)
            turn_rows(base, job + 1, 1, 1)
            project(base, job + 2)


def kernel(**inputs):
    import numpy as np

    import concourse.bacc as bacc
    from concourse.bass_utils import run_bass_kernel_spmd

    def f(name):
        return np.asarray(inputs[name])

    def by_group(a):
        return np.ascontiguousarray(a.reshape(a.shape[:-1] + (NG, HG, DH)).swapaxes(-1, -2).reshape(a.shape))

    wv = np.concatenate([f("L0_attn_Wv"), f("L0_attn_bv")[None, :]], 0)
    wgu = f("L0_ffn_Wgu").reshape(NEXP, D, P, 2).swapaxes(2, 3).reshape(NEXP, D, 2 * P)
    wexp = np.concatenate([wgu, f("L0_ffn_bgu").reshape(NEXP, P, 2), f("L0_ffn_Wd")], 2)
    bdo = np.zeros((33, D), np.float32)
    bdo[:NEXP] = f("L0_ffn_bd")
    bdo[32] = f("L0_attn_bo")
    arrays = {
        "x": f("L0_attn_x"), "wq": by_group(f("L0_attn_Wq")), "bq": by_group(f("L0_attn_bq"))[:, None],
        "wl": f("L0_attn_Wl"), "bl": f("L0_attn_bl")[:, None], "wk": by_group(f("L0_attn_Wk")),
        "bk": by_group(f("L0_attn_bk"))[:, None], "wv": wv, "wo": f("L0_attn_Wo"),
        "wg": f("L0_ffn_Wg").T, "bg": f("L0_ffn_bg")[None, :], "wexp": wexp, "bdo": bdo,
        "ident": np.eye(P, dtype=np.float32), 
        "iota": np.tile(np.arange(BLOCKS, dtype=np.float32), (P, 1)),
        "before": np.triu(np.ones((P, P), np.float32), 1),
    }
    arrays = {n: np.ascontiguousarray(a) for n, a in arrays.items()}
    nc = bacc.Bacc("TRN2", target_bir_lowering=False, num_devices=1)
    args = [nc.dram_tensor(f"in_{n}", a.shape, F32, kind="ExternalInput").ap() for n, a in arrays.items()]
    out = nc.dram_tensor("out", (B, S, D), F32, kind="ExternalOutput").ap()
    moe_attention_kernel(nc, *args, out)
    r = run_bass_kernel_spmd(nc, [{f"in_{n}": a for n, a in arrays.items()}], core_ids=[0])
    return r.results[0]["out"]
```
